# Optimizing a Trainium2 kernel written in Bass

```python
import numpy as np
import jax
import jax.numpy as jnp

def _softmax(x, axis=-1):
    return jax.nn.softmax(x, axis=axis)

def _gelu(x):
    return jax.nn.gelu(x, approximate=True)

def _silu(x):
    return jax.nn.silu(x)

def _sigmoid(x):
    return jax.nn.sigmoid(x)

def _layernorm(x, axis=-1, eps=1e-05):
    m = jnp.mean(x, axis=axis, keepdims=True)
    v = jnp.var(x, axis=axis, keepdims=True)
    return (x - m) / jnp.sqrt(v + eps)

def _scatter_add(tgt, idx, src, axis=0):
    return tgt.at[idx].add(src)

def _segment_sum(src, seg, n):
    return jax.ops.segment_sum(src, seg, n)
kernel_name = 'mk_xattn_ffn_d1_seqx_r4_57e658'

def setup_inputs(seed: int=0):
    np.random.seed(seed)
    _w = jnp.asarray

    def _rec_inputs():
        import jax
        import jax.numpy as jnp
        _rk = jax.random.key(seed)
        x = -0.0002928 + 1 * jax.random.normal(jax.random.fold_in(_rk, 1), (4, 512, 256), jnp.float32)
        _lenS = 512 - jax.random.randint(jax.random.fold_in(_rk, 7), (4,), 0, max(1, 512 // 4) + 1, jnp.int32)
        _lenS2 = 1601 - jax.random.randint(jax.random.fold_in(_rk, 8), (4,), 0, max(1, 1601 // 4) + 1, jnp.int32)
        _ctx_1024P = jax.random.normal(jax.random.fold_in(_rk, 11), (4, 16, 256), jnp.float32)
        _ctx_1024c = jax.random.dirichlet(jax.random.fold_in(_rk, 511), 0.3 * jnp.ones((16,), jnp.float32), (4, 1601))
        _ctx_1024t = jnp.einsum('bsk,bkd->bsd', _ctx_1024c, _ctx_1024P)
        _ctx_1024t = _ctx_1024t * jax.lax.rsqrt(jnp.mean(jnp.square(_ctx_1024t)) + 1e-12) * 0.953939
        ctx_1024 = -1.39393e-06 + 0.999914 * (_ctx_1024t + 0.3 * jax.random.normal(jax.random.fold_in(_rk, 611), (4, 1601, 256), jnp.float32))
        return (x, ctx_1024)
    x, ctx_1024 = _rec_inputs()

    def _L0_xattn_setup():
        import jax, jax.numpy as jnp
        import numpy as np
        D_MODEL = 256
        NUM_HEADS = 16
        D_K = D_MODEL // NUM_HEADS
        key = jax.random.key(seed)
        ks = jax.random.split(key, 11)
        B, S, D = (2, 512, D_MODEL)
        s = 1.0 / np.sqrt(D)
        return {'query': jax.random.normal(ks[0], (B, S, D), jnp.float32), 'key': jax.random.normal(ks[1], (B, S, D), jnp.float32), 'value': jax.random.normal(ks[2], (B, S, D), jnp.float32), 'Wq': jax.random.normal(ks[3], (D, D), jnp.float32) * s, 'bq': jnp.zeros((D,), jnp.float32), 'Wk': jax.random.normal(ks[4], (D, D), jnp.float32) * s, 'bk': jnp.zeros((D,), jnp.float32), 'Wv': jax.random.normal(ks[5], (D, D), jnp.float32) * s, 'bv': jnp.zeros((D,), jnp.float32), 'Wo': jax.random.normal(ks[6], (D, D), jnp.float32) * s, 'bo': jnp.zeros((D,), jnp.float32)}
    _L0_xattn_all = _L0_xattn_setup()
    _L0_xattn_in = {k: v for k, v in _L0_xattn_all.items() if k in ('Wq', 'bq', 'Wk', 'bk', 'Wv', 'bv', 'Wo', 'bo')}
    del _L0_xattn_all

    def _L0_ffn_setup():
        import jax, jax.numpy as jnp
        import numpy as np
        B, T, D = (4, 1024, 256)
        E = 8
        TOP_K = 2
        FFN = 768
        HALF = FFN // 2

        def _kaiming_uniform(key, shape, fan_in):
            bound = 1.0 / np.sqrt(fan_in)
            return jax.random.uniform(key, shape, jnp.float32, -bound, bound)
        key = jax.random.key(seed)
        ks = jax.random.split(key, 7)
        x = jax.random.normal(ks[0], (B, T, D), jnp.float32)
        gate_w = _kaiming_uniform(ks[1], (E, D), D) * 0.01
        w_up = _kaiming_uniform(ks[2], (E, FFN, D), D)
        w_down = _kaiming_uniform(ks[3], (E, D, HALF), HALF)
        sg_gate = _kaiming_uniform(ks[4], (HALF, D), D)
        sg_up = _kaiming_uniform(ks[5], (HALF, D), D)
        sg_down = _kaiming_uniform(ks[6], (D, HALF), HALF)
        return {'x': x, 'gate_w': gate_w, 'w_up': w_up, 'w_down': w_down, 'sg_gate': sg_gate, 'sg_up': sg_up, 'sg_down': sg_down}
    _L0_ffn_all = _L0_ffn_setup()
    _L0_ffn_in = {k: v for k, v in _L0_ffn_all.items() if k in ('gate_w', 'w_up', 'w_down', 'sg_gate', 'sg_up', 'sg_down')}
    del _L0_ffn_all
    return {'x': x, 'ctx_1024': ctx_1024, 'L0_xattn_Wq': _L0_xattn_in['Wq'], 'L0_xattn_bq': _L0_xattn_in['bq'], 'L0_xattn_Wk': _L0_xattn_in['Wk'], 'L0_xattn_bk': _L0_xattn_in['bk'], 'L0_xattn_Wv': _L0_xattn_in['Wv'], 'L0_xattn_bv': _L0_xattn_in['bv'], 'L0_xattn_Wo': _L0_xattn_in['Wo'], 'L0_xattn_bo': _L0_xattn_in['bo'], 'L0_ffn_gate_w': _L0_ffn_in['gate_w'], 'L0_ffn_w_up': _L0_ffn_in['w_up'], 'L0_ffn_w_down': _L0_ffn_in['w_down'], 'L0_ffn_sg_gate': _L0_ffn_in['sg_gate'], 'L0_ffn_sg_up': _L0_ffn_in['sg_up'], 'L0_ffn_sg_down': _L0_ffn_in['sg_down']}

def reference(x, ctx_1024, L0_xattn_Wq, L0_xattn_bq, L0_xattn_Wk, L0_xattn_bk, L0_xattn_Wv, L0_xattn_bv, L0_xattn_Wo, L0_xattn_bo, L0_ffn_gate_w, L0_ffn_w_up, L0_ffn_w_down, L0_ffn_sg_gate, L0_ffn_sg_up, L0_ffn_sg_down):
    import jax
    import jax.numpy as jnp

    def _L0_xattn_ref(query, key, value, Wq, bq, Wk, bk, Wv, bv, Wo, bo):
        import jax, jax.numpy as jnp
        import numpy as np
        D_MODEL = 256
        NUM_HEADS = 16
        D_K = D_MODEL // NUM_HEADS
        B, Sq, D = query.shape
        Sk = key.shape[1]
        H, dk = (NUM_HEADS, D_K)
        Q = (query @ Wq.T + bq).reshape(B, Sq, H, dk).transpose(0, 2, 1, 3)
        K = (key @ Wk.T + bk).reshape(B, Sk, H, dk).transpose(0, 2, 1, 3)
        V = (value @ Wv.T + bv).reshape(B, Sk, H, dk).transpose(0, 2, 1, 3)
        scores = jnp.einsum('bhqd,bhkd->bhqk', Q, K) / jnp.sqrt(jnp.float32(dk))
        causal = jnp.tril(jnp.ones((Sq, Sk), dtype=bool))
        scores = jnp.where(causal, scores, -jnp.inf)
        attn = jax.nn.softmax(scores, axis=-1)
        out = jnp.einsum('bhqk,bhkd->bhqd', attn, V)
        out = out.transpose(0, 2, 1, 3).reshape(B, Sq, D)
        return out @ Wo.T + bo

    def _L0_ffn_ref(x, gate_w, w_up, w_down, sg_gate, sg_up, sg_down):
        import jax, jax.numpy as jnp
        import numpy as np
        B, T, D = (4, 1024, 256)
        E = 8
        TOP_K = 2
        FFN = 768
        HALF = FFN // 2

        def _kaiming_uniform(key, shape, fan_in):
            bound = 1.0 / np.sqrt(fan_in)
            return jax.random.uniform(key, shape, jnp.float32, -bound, bound)
        b, t, d = x.shape
        xf = x.reshape(b * t, d)
        N = xf.shape[0]
        logits = xf @ gate_w.T
        topk_logits, topk_idx = jax.lax.top_k(logits, TOP_K)
        topk_w = jax.nn.softmax(topk_logits.astype(jnp.float32), axis=-1).astype(x.dtype)
        comb = jnp.zeros((N, E), x.dtype).at[jnp.arange(N)[:, None], topk_idx].add(topk_w)
        wg = w_up[:, :HALF, :]
        wu = w_up[:, HALF:, :]
        out = jnp.zeros_like(xf)
        for e in range(E):
            g = xf @ wg[e].T
            u = xf @ wu[e].T
            y = jax.nn.silu(g) * u @ w_down[e].T
            out = out + comb[:, e:e + 1] * y
        shared = jax.nn.silu(xf @ sg_gate.T) * (xf @ sg_up.T) @ sg_down.T
        return (shared + out).reshape(b, t, d)
    x = x + _L0_xattn_ref(_layernorm(x, axis=-1), ctx_1024, ctx_1024, L0_xattn_Wq, L0_xattn_bq, L0_xattn_Wk, L0_xattn_bk, L0_xattn_Wv, L0_xattn_bv, L0_xattn_Wo, L0_xattn_bo)
    x = x + _L0_ffn_ref(_layernorm(x, axis=-1), L0_ffn_gate_w, L0_ffn_w_up, L0_ffn_w_down, L0_ffn_sg_gate, L0_ffn_sg_up, L0_ffn_sg_down)
    return x

_drawn_inputs = setup_inputs


def setup_inputs(seed=0):
    import zlib

    import numpy as np

    out = dict(_drawn_inputs(seed))
    spreads = {'L0_xattn_bq': (0.0, 0.309),
     'L0_xattn_bk': (0.0, 0.8),
     'L0_xattn_bv': (0.0, 0.1),
     'L0_xattn_bo': (0.0, 0.1)}
    factors = {}
    for name, (base, spread) in spreads.items():
        noise = np.random.default_rng([zlib.crc32(name.encode()), seed]).standard_normal(out[name].shape)
        drawn = base * np.exp(spread * noise) if base else spread * noise
        out[name] = jnp.asarray(drawn.astype(out[name].dtype))
    for name, factor in factors.items():
        out[name] = (out[name] * factor).astype(out[name].dtype)
    return out
```

```python
from contextlib import ExitStack

import concourse.bass as bass
from concourse import mybir

P = 128
F32 = mybir.dt.float32
BF16 = mybir.dt.bfloat16
I32 = mybir.dt.int32
ALU = mybir.AluOpType
ACT = mybir.ActivationFunctionType
AX = mybir.AxisListType

NUM_HEADS = 16
EPS = 1e-5
MASKED = -1e30
LOWEST = -3e38
DMA = 16


def build(nc, x, ctxT, wqT, bq, wkT, bk, wvT, bv, woT, bo, gwT, wupT, wdnT, sgT, suT, sdT, out):
    B, S, D = x.shape
    H = NUM_HEADS
    DK = D // H
    HG = P // 32
    NG = H // HG
    C = D // P
    QT = S // P
    N = B * S
    T = N // P
    E = gwT.shape[1]
    HALF = sgT.shape[1]
    M = HALF // P
    TOP_K = 2
    NT = (TOP_K * N + E * (P - 1)) // P
    NT += NT % 2
    SCALE = float(DK) ** -0.5
    assert S == 512 and D == 256 and HG * 32 == P

    with ExitStack() as ctx:
        def sb(name, shape, dt=F32):
            return ctx.enter_context(nc.sbuf_tensor(name, shape, dt))

        def sem(name):
            return ctx.enter_context(nc.semaphore(name))

        xg = nc.dram_tensor("x_by_slot", (NT * P, D), F32, kind="Internal").ap()
        yg = nc.dram_tensor("y_by_slot", (NT * P, D), F32, kind="Internal").ap()

        A = ctx.enter_context(nc.psum_tensor("set_a", [P, 4, 512], F32))
        Bk = ctx.enter_context(nc.psum_tensor("set_b", [P, 4, 512], F32))

        xs_all = sb("x_res", [P, T, D])
        wup = sb("w_up", [P, C, E * 2 * HALF])
        wdn = sb("w_down", [P, M, E * D])
        wsg = sb("w_sg", [P, C, HALF])
        wsu = sb("w_su", [P, C, HALF])
        wsd = sb("w_sd", [P, M, D])
        gw = sb("gate_w", [P, C, E])
        ident = sb("ident", [P, P])
        identb = sb("identb", [P, P], BF16)
        maskb = sb("maskb", [P, P], BF16)
        beforeb = sb("beforeb", [P, P], BF16)
        onesb = sb("onesb", [P, P], BF16)
        slots = sb("slots", [P, TOP_K, T], I32)
        wts = sb("wts", [P, TOP_K, T])
        expert_of = sb("expert_of", [P, NT], I32)
        stats = sb("stats", [P, T, 6])
        st_a = sb("st_a", [P, T])
        st_b = sb("st_b", [P, T])
        st_c = sb("st_c", [P, T])
        mean = sb("mean", [P, T])
        rstd = sb("rstd", [P, T])
        std = sb("std", [P, T])

        credit = sb("credit", [P, 4])

        KB = 256
        REGION = 107 * KB
        region = sb("region", [P, REGION])
        used = [0]

        def part(words, restart=False):
            if restart:
                used[0] = 0
            lo = used[0]
            used[0] += words
            assert used[0] <= REGION, used[0] / KB
            return region[:, lo:lo + words]

        xnT = part(C * N).rearrange("p (c n) -> p c n", c=C)
        cT = part(C * N).rearrange("p (c n) -> p c n", c=C)
        pT_at = [sum(HG * (S - P * j) for j in range(k)) for k in range(QT + 1)]
        pT_all = part(pT_at[QT])
        pT = [pT_all[:, pT_at[k]:pT_at[k + 1]].rearrange("p (h q) -> p h q", h=HG) for k in range(QT)]
        kT = part(2 * S).rearrange("p (a n) -> p a n", a=2)
        qT = part(S)
        qaT = part(2 * S).rearrange("p (a n) -> p a n", a=2)
        vaug = part(QT * H * 32).rearrange("p (k h w) -> p k h w", k=QT, h=H)
        oT = part(NG * S).rearrange("p (g n) -> p g n", g=NG)
        attn = part(QT * D).rearrange("p (k d) -> p k d", k=QT)
        attnT = part(C * S).rearrange("p (c n) -> p c n", c=C)
        cV = part(C * S).rearrange("p (c n) -> p c n", c=C)
        wq = part(C * NG * P).rearrange("p (c n) -> p c n", c=C)
        wk = part(C * NG * P).rearrange("p (c n) -> p c n", c=C)
        wv = part(C * D).rearrange("p (c n) -> p c n", c=C)
        wo = part(C * D).rearrange("p (c n) -> p c n", c=C)
        bv_bc = part(D)
        mz = part(QT * P).rearrange("p (k n) -> p k n", k=QT)
        rc = part(QT * H).rearrange("p (k h) -> p k h", k=QT)
        bqc = part(NG)
        bkc = part(NG)
        ones_row = part(1)
        xs = attn
        wq_raw = oT[:, 0, :].rearrange("p (c n) -> p c n", c=C)
        wk_raw = oT[:, 1, :].rearrange("p (c n) -> p c n", c=C)
        bo_bc = oT[:, 2, 0:D]
        zeros = oT[:, 3, 0:D]

        xn2 = part(T * D, restart=True).rearrange("p (t d) -> p t d", t=T)
        xn2T = part(C * N).rearrange("p (c n) -> p c n", c=C)
        xs2 = part(QT * D).rearrange("p (k d) -> p k d", k=QT)
        xTs = part(C * S).rearrange("p (c n) -> p c n", c=C)
        sg = part(M * S).rearrange("p (m n) -> p m n", m=M)
        hT = part(M * S).rearrange("p (m n) -> p m n", m=M)
        TE = T * E

        def te():
            return part(TE).rearrange("p (t e) -> p t e", e=E)

        lg, io, io8, oh1, oh2, ra, rb, rslot = (te() for _ in range(8))
        selb = part(TE // 2).bitcast(BF16).rearrange("p (t e) -> p t e", e=E)
        m1, m2, i1, i2, dl, ex, sm = (part(T) for _ in range(7))
        k128 = part(E * T).rearrange("p (e k) -> p e k", e=E)
        upto = part(E * E).rearrange("p (a b) -> p a b", a=E)
        tot, tiles_of, ends, base = (part(E) for _ in range(4))
        ee = part(E * E).rearrange("p (a b) -> p a b", a=E)
        tio = part(NT * E).rearrange("p (t e) -> p t e", e=E)
        tcmp = part(NT * E).rearrange("p (t e) -> p t e", e=E)
        tnum = part(NT)
        slotf = part(TOP_K * T).rearrange("p (k t) -> p k t", k=TOP_K)
        e_x = part(2 * D).rearrange("p (a d) -> p a d", a=2)
        e_xT = part(2 * C * P).rearrange("p (a c n) -> p a c n", a=2, c=C)
        e_sg = part(2 * HALF).rearrange("p (a d) -> p a d", a=2)
        e_h = part(2 * HALF).rearrange("p (a d) -> p a d", a=2)
        e_hT = part(2 * M * P).rearrange("p (a c n) -> p a c n", a=2, c=M)
        e_y = part(2 * D).rearrange("p (a d) -> p a d", a=2)
        NYB = 4
        yb = part(NYB * TOP_K * D).rearrange("p (a k d) -> p a k d", a=NYB, k=TOP_K)

        ld_x = [sem(f"ld_x{b}") for b in range(B)]
        ld_wqk, ld_b, ld_ctx, ld_wvo, ld_cv, ld_moe = (sem(n) for n in
            ("ld_wqk", "ld_b", "ld_ctx", "ld_wvo", "ld_cv", "ld_moe"))
        zero_ready, xg_zeroed = sem("zero_ready"), sem("xg_zeroed")
        consts, pads, pads_set = sem("consts"), sem("pads"), sem("pads_set")
        st_done, ln_step, std_ready, xs_ready = sem("st_done"), sem("ln_step"), sem("std_ready"), sem("xs_ready")
        mean_done, kept, pads_dve, q_kept = sem("mean_done"), sem("kept"), sem("pads_dve"), sem("q_kept")
        bo_added = sem("bo_added")
        a_full, a_free, b_full, b_free = sem("a_full"), sem("a_free"), sem("b_full"), sem("b_free")
        p_masked, rc_ready, mask_turn = sem("p_masked"), sem("rc_ready"), sem("mask_turn")
        xT_kept, route, d_ready, ex_ready, sel_ready, rank_full, slots_ready = (sem(n) for n in
            ("xT_kept", "route", "d_ready", "ex_ready", "sel_ready", "rank_full", "slots_ready"))
        rconsts, scattered = sem("rconsts"), sem("scattered")
        s_up, s_sg, s_h, s_y, s_yfree = (sem(n) for n in ("s_up", "s_sg", "s_h", "s_y", "s_yfree"))
        e_in = [sem("e_in0"), sem("e_in1")]
        e_out = [sem("e_out0"), sem("e_out1")]
        e_xt, e_xTr, e_up, e_sgr, e_hr, e_ht, e_hTr, e_yf, e_yr = (sem(n) for n in
            ("e_xt", "e_xTr", "e_up", "e_sgr", "e_hr", "e_ht", "e_hTr", "e_yf", "e_yr"))
        y_in = [sem(f"y_in{i}") for i in range(NYB)]
        comb1, comb2, stored = sem("comb1"), sem("comb2"), sem("stored")

        A_PRO = QT + 2
        A_PER = 1 + NG * (QT + 2) + 2
        A_LOGITS = A_PRO + B * A_PER - (QT + 2)
        B_PER = NG * (QT + 1) + 1
        B_ATT = B
        B_LN2 = B + B * B_PER

        block = ctx.enter_context(nc.Block())

        @block.sync
        def _(sp):
            x_t = x.rearrange("b (k p) d -> b p k d", p=P)
            for b in range(B):
                sp.dma_start(xs_all[:, b * QT:(b + 1) * QT, :], x_t[b]).then_inc(ld_x[b], DMA)
            sp.dma_start(wq_raw, wqT.rearrange("(c p) n -> p c n", p=P)).then_inc(ld_wqk, DMA)
            sp.dma_start(wk_raw, wkT.rearrange("(c p) n -> p c n", p=P)).then_inc(ld_wqk, DMA)
            for b in range(B):
                sp.dma_start(cT[:, :, b * S:(b + 1) * S],
                             ctxT[b].rearrange("(c p) n -> p c n", p=P)[:, :, 0:S]).then_inc(ld_ctx, DMA)
            sp.dma_start(wv, wvT.rearrange("(c p) n -> p c n", p=P)).then_inc(ld_wvo, DMA)
            sp.dma_start(wo, woT.rearrange("(c p) n -> p c n", p=P)).then_inc(ld_wvo, DMA)
            sp.dma_start(bv_bc, bv.partition_broadcast(P)).then_inc(ld_wvo, DMA)
            sp.dma_start(bo_bc, bo.partition_broadcast(P)).then_inc(ld_b, DMA)
            sp.wait_ge(zero_ready, 1)
            sp.dma_start(xg.rearrange("(t p) d -> p t d", p=P),
                         zeros.rearrange("p (o d) -> p o d", o=1).to_broadcast([P, NT, D])).then_inc(xg_zeroed, DMA)
            sp.dma_start(cV, ctxT[0].rearrange("(c p) n -> p c n", p=P)[:, :, 0:S]).then_inc(ld_cv, DMA)
            sp.dma_start(wsg[:], sgT.rearrange("(c p) n -> p c n", p=P)).then_inc(ld_moe, DMA)
            sp.dma_start(wsu[:], suT.rearrange("(c p) n -> p c n", p=P)).then_inc(ld_moe, DMA)
            sp.dma_start(wsd[:], sdT.rearrange("(c p) n -> p c n", p=P)).then_inc(ld_moe, DMA)
            sp.dma_start(gw[:], gwT.rearrange("(c p) n -> p c n", p=P)).then_inc(ld_moe, DMA)
            for c in range(C):
                sp.dma_start(wup[:, c, :], wupT[c * P:(c + 1) * P]).then_inc(ld_moe, DMA)
            for m in range(M):
                sp.dma_start(wdn[:, m, :], wdnT[m * P:(m + 1) * P]).then_inc(ld_moe, DMA)
            for b in range(1, B):
                sp.wait_ge(a_full, A_PRO + (b - 1) * A_PER + 1)
                sp.dma_start(cV, ctxT[b].rearrange("(c p) n -> p c n", p=P)[:, :, 0:S]).then_inc(ld_cv, DMA)

            xg_t = xg.rearrange("(t p) d -> t p d", p=P)
            yg_t = yg.rearrange("(t p) d -> t p d", p=P)
            sp.wait_ge(scattered, DMA * TOP_K * T)
            for a in range(2):
                sp.dma_start(e_x[:, a, :], xg_t[a]).then_inc(e_in[a], DMA)
            with sp.Fori(0, NT // 2 - 1) as i:
                for a in range(2):
                    sp.wait_ge(e_xt, 2 * i + a + 1)
                    sp.dma_start(e_x[:, a, :], xg[bass.ds((2 * i + 2 + a) * P, P), :]).then_inc(e_in[a], DMA)
                    sp.wait_ge(e_yr, 2 * i + a + 2)
                    sp.dma_start(yg[bass.ds((2 * i + a) * P, P), :], e_y[:, a, :]).then_inc(e_out[a], DMA)
            for t in range(NT - 2, NT):
                sp.wait_ge(e_yr, t + 2)
                sp.dma_start(yg_t[t], e_y[:, t % 2, :]).then_inc(e_out[t % 2], DMA)

            o_t = out.rearrange("b (k p) d -> (b k) p d", p=P)
            for t in range(T):
                sp.wait_ge(comb2, t + 1)
                sp.dma_start(o_t[t], xs_all[:, t, :]).then_inc(stored, DMA)
            sp.wait_ge(stored, DMA * T)

        @block.gpsimd
        def _(pool):
            g = nc.gpsimd
            g.memset(zeros, 0.0).then_inc(zero_ready, 1)
            g.memset(ident[:], 0.0).then_inc(pads, 1)
            g.memset(identb[:], 0.0).then_inc(pads, 1)
            g.memset(maskb[:], 0.0).then_inc(pads, 1)
            g.memset(beforeb[:], 0.0).then_inc(pads, 1)
            g.memset(wq, 0.0).then_inc(pads, 1)
            g.memset(wk, 0.0).then_inc(pads, 1)
            g.memset(bqc, 0.0).then_inc(pads, 1)
            g.memset(bkc, 0.0).then_inc(pads, 1)
            g.memset(mz, 0.0).then_inc(pads, 1)
            g.memset(vaug, 1.0).then_inc(pads, 1)
            g.memset(onesb[:], 1.0).then_inc(pads, 1)
            g.memset(credit[:, 0:1], 0.0).then_inc(s_yfree, 1)
            g.memset(credit[:, 1:2], 0.0).then_inc(e_yr, 1)
            g.memset(credit[:, 2:3], 0.0).then_inc(e_out[0], DMA)
            g.memset(credit[:, 3:4], 0.0).then_inc(e_out[1], DMA)
            pool.wait_ge(pads, 11)
            g.affine_select(out=ident[:], in_=ident[:], compare_op=ALU.not_equal, fill=1.0, base=0,
                            pattern=[[-1, P]], channel_multiplier=1).then_inc(consts, 1)
            g.affine_select(out=identb[:], in_=identb[:], compare_op=ALU.not_equal, fill=1.0, base=0,
                            pattern=[[-1, P]], channel_multiplier=1).then_inc(consts, 1)
            g.affine_select(out=maskb[:], in_=maskb[:], compare_op=ALU.is_ge, fill=MASKED, base=0,
                            pattern=[[-1, P]], channel_multiplier=1).then_inc(consts, 1)
            g.affine_select(out=beforeb[:], in_=beforeb[:], compare_op=ALU.is_ge, fill=1.0, base=0,
                            pattern=[[-1, P]], channel_multiplier=1).then_inc(consts, 1)
            for b_dram, col in ((bq, bqc), (bk, bkc)):
                for h in range(HG):
                    pool.dma_start(col[32 * h:32 * h + DK, :], b_dram[h]).then_inc(pads_set, DMA)
            pool.wait_ge(ld_wqk, 2 * DMA)
            for w, raw in ((wq, wq_raw), (wk, wk_raw)):
                g.tensor_copy(w.rearrange("p c (h w) -> p c h w", w=32)[:, :, :, 0:DK],
                              raw.rearrange("p c (h i) -> p c h i", i=DK)).then_inc(consts, 1)
            pool.wait_ge(ld_b, DMA)
            pool.wait_ge(xs_ready, B)
            g.tensor_tensor(xs_all[:], xs_all[:],
                            bo_bc.rearrange("p (o d) -> p o d", o=1).to_broadcast([P, T, D]),
                            ALU.add).then_inc(bo_added, 1)

            def mask_batch(b):
                for s in range(NG):
                    for k in range(QT):
                        pool.wait_ge(b_free, B_ATT + b * B_PER + s * (QT + 1) + k + 2)
                        pool.sem_inc(mask_turn)
                        diag = pT[k][:, :, 0:P]
                        g.affine_select(out=diag, in_=diag, compare_op=ALU.is_ge, fill=0.0, base=0,
                                        pattern=[[0, HG], [1, P]], channel_multiplier=-1).then_inc(p_masked, 1)

            with pool.Fori(0, B) as b:
                mask_batch(b)

            pool.wait_ge(a_free, A_LOGITS)
            g.iota(io, [[0, T], [1, E]], base=0, channel_multiplier=0,
                   allow_small_or_imprecise_dtypes=True).then_inc(rconsts, 1)
            g.iota(io8, [[0, T], [1, E]], base=E, channel_multiplier=0,
                   allow_small_or_imprecise_dtypes=True).then_inc(rconsts, 1)
            g.iota(k128, [[0, E], [P, T]], base=0, channel_multiplier=0,
                   allow_small_or_imprecise_dtypes=True).then_inc(rconsts, 1)
            g.iota(tio, [[1, NT], [0, E]], base=0, channel_multiplier=0,
                   allow_small_or_imprecise_dtypes=True).then_inc(rconsts, 1)
            g.memset(upto, 1.0).then_inc(rconsts, 1)
            pool.wait_ge(rconsts, 5)
            g.affine_select(out=upto, in_=upto, compare_op=ALU.is_ge, fill=0.0, base=0,
                            pattern=[[1, E], [-1, E]], channel_multiplier=0).then_inc(rconsts, 1)

            pool.wait_ge(xg_zeroed, DMA)
            pool.wait_ge(slots_ready, TOP_K)
            for t in range(T):
                for k in range(TOP_K):
                    g.indirect_dma_start(xg, bass.IndirectOffsetOnAxis(slots[:, k, t:t + 1], 0),
                                         xn2[:, t, :], None).then_inc(scattered, DMA)
            for a in range(2):
                pool.wait_ge(e_out[a], DMA * (NT // 2 + 1))
            for t in range(T):
                if t >= NYB:
                    pool.wait_ge(comb2, t - NYB + 1)
                for k in range(TOP_K):
                    g.indirect_dma_start(yb[:, t % NYB, k, :], None, yg,
                                         bass.IndirectOffsetOnAxis(slots[:, k, t:t + 1], 0)
                                         ).then_inc(y_in[t % NYB], DMA)

        @block.tensor
        def _(pe):
            mm, tr = nc.tensor.matmul, nc.tensor.transpose

            def ln_transposes(b, base, stage):
                pe.wait_ge(xs_ready, (b + 1) if base == 0 else (b + 1 + B))
                pe.wait_ge(b_free, base + b + 1)
                for c in range(C):
                    for j in range(QT):
                        last = tr(Bk[:, c, j * P:(j + 1) * P], stage[:, j, c * P:(c + 1) * P], ident[:])
                last.then_inc(b_full, 1)

            pe.wait_ge(consts, 4)
            with pe.Fori(0, B) as b:
                ln_transposes(b, 0, xs)

            def qk(b, g, n):
                pe.wait_ge(a_free, n)
                for w, bank, src in ((wq, 0, xnT), (wk, 1, cT)):
                    for c in range(C):
                        last = mm(A[:, bank, :], w[:, c, g * P:(g + 1) * P], src[:, c, bass.ds(b * S, S)],
                                  start=c == 0, stop=c == C - 1)
                last.then_inc(a_full, 1)

            def rowmax_scores(g, k, n):
                pe.wait_ge(a_free, n)
                w = (k + 1) * P
                for h in range(HG):
                    r = slice(32 * h, 32 * h + 32)
                    mm(A[:, h, 0:w], qT[r, k * P:w], kT[r, g % 2, 0:w], start=True, stop=False,
                       tile_position=(32 * h, 0))
                for h in range(HG):
                    last = mm(A[:, h, k * P:w], identb[:], maskb[:], start=False, stop=True)
                last.then_inc(a_full, 1)

            def maxima(n):
                pe.wait_ge(a_free, n)
                for k in range(QT):
                    last = tr(A[:, 0, k * P:(k + 1) * P], mz[:, k, :], ident[:])
                last.then_inc(a_full, 1)

            def scoresT(g, k, n):
                pe.wait_ge(b_free, n + 1)
                for h in range(HG):
                    r = slice(32 * h, 32 * h + 32)
                    last = mm(Bk[:, h, 0:S - k * P], kT[r, g % 2, k * P:(k + 1) * P], qaT[r, g % 2, k * P:S],
                              start=True, stop=True, tile_position=(32 * h, 0))
                last.then_inc(b_full, 1)

            def probs_v(b, g, n):
                pe.wait_ge(b_free, n + 1)
                for k in range(QT):
                    pe.wait_ge(p_masked, (b * NG + g) * QT + k + 1)
                    for h in range(HG):
                        last = mm(Bk[32 * h:32 * h + 32, 0, k * P:S], vaug[:, k, HG * g + h, :], pT[k][:, h, :],
                                  start=k == 0, stop=k == QT - 1, tile_position=(0, 32 * h))
                last.then_inc(b_full, 1)

            pe.wait_ge(b_free, B + 1)
            pe.wait_ge(consts, 6)
            pe.wait_ge(ld_ctx, DMA * B)
            pe.wait_ge(ld_wvo, DMA * 3)
            for c in range(C):
                mm(A[:, 0, :], wq[:, c, 0:P], xnT[:, c, 0:S], start=c == 0, stop=c == C - 1)
            for c in range(C):
                last = mm(A[:, 1, :], wk[:, c, 0:P], cT[:, c, 0:S], start=c == 0, stop=c == C - 1)
            last.then_inc(a_full, 1)
            for k in range(QT):
                rowmax_scores(0, k, k + 1)
            maxima(QT + 1)

            def batch(b, final):
                n_a = A_PRO + b * A_PER
                n_b = B_ATT + b * B_PER
                pe.wait_ge(a_free, n_a)
                pe.wait_ge(ld_cv, DMA * (b + 1))
                for k in range(QT):
                    for c in range(C):
                        last = mm(A[:, k // 2, (k % 2) * D:(k % 2 + 1) * D], cV[:, c, k * P:(k + 1) * P],
                                  wv[:, c, :], start=c == 0, stop=c == C - 1)
                last.then_inc(a_full, 1)
                n_a = n_a + 1
                for s in range(NG):
                    ahead = not (final and s == NG - 1)
                    g1 = (s + 1) % NG
                    if ahead:
                        qk(b + 1 if s == NG - 1 else b, g1, n_a)
                    else:
                        pe.wait_ge(a_free, n_a)
                    for k in range(QT):
                        scoresT(s, k, n_b + k)
                        if ahead:
                            rowmax_scores(g1, QT - 1 - k, n_a + 1 + k)
                    probs_v(b, s, n_b + QT)
                    n_b = n_b + QT + 1
                    if ahead:
                        maxima(n_a + QT + 1)
                        n_a = n_a + QT + 2
                pe.wait_ge(a_free, n_a)
                pe.wait_ge(b_free, n_b + 1)
                for k in range(QT):
                    for g in range(NG):
                        last = tr(A[:, k, g * P:(g + 1) * P], oT[:, g, k * P:(k + 1) * P], ident[:])
                last.then_inc(a_full, 1)
                pe.wait_ge(a_free, n_a + 1)
                for c in range(C):
                    for k in range(QT):
                        last = tr(Bk[:, c, k * P:(k + 1) * P], attn[:, k, c * P:(c + 1) * P], ident[:])
                last.then_inc(b_full, 1)
                pe.wait_ge(b_free, n_b + 2)
                for k in range(QT):
                    for c in range(C):
                        last = mm(A[:, k // 2, (k % 2) * D:(k % 2 + 1) * D], attnT[:, c, k * P:(k + 1) * P],
                                  wo[:, c, :], start=c == 0, stop=c == C - 1)
                last.then_inc(a_full, 1)

            with pe.Fori(0, B - 1) as b:
                batch(b, False)
            batch(B - 1, True)

            pe.wait_ge(a_free, A_LOGITS)
            pe.wait_ge(ld_moe, DMA * (4 + C + M))
            with pe.Fori(0, B) as b:
                ln_transposes(b, B_LN2, xs2)
                pe.wait_ge(b_free, B_LN2 + b + 2)
                for j in range(QT):
                    for c in range(C):
                        last = mm(A[:, 0, bass.ds((b * QT + j) * E, E)], xTs[:, c, j * P:(j + 1) * P], gw[:, c, :],
                                  start=c == 0, stop=c == C - 1)
                last.then_inc(a_full, 1)

            gu = [(A[:, 0, :], A[:, 1, :]), (A[:, 2, :], A[:, 3, :]), (Bk[:, 0, :], Bk[:, 1, :])]

            def shared_up(b):
                for m in range(M):
                    for w, dst in zip((wsg, wsu), gu[m]):
                        for c in range(C):
                            last = mm(dst, w[:, c, m * P:(m + 1) * P], xn2T[:, c, bass.ds(b * S, S)],
                                      start=c == 0, stop=c == C - 1)
                    last.then_inc(s_up, 1)

            def shared_down(b):
                pe.wait_ge(s_yfree, b + 1)
                for m in range(M):
                    pe.wait_ge(s_h, b * M + m + 1)
                    for j in range(QT):
                        last = mm(Bk[:, 2 + j // 2, (j % 2) * D:(j % 2 + 1) * D], hT[:, m, j * P:(j + 1) * P],
                                  wsd[:, m, :], start=m == 0 and j % 2 == 0, stop=m == M - 1,
                                  skip_group_check=True)
                last.then_inc(s_y, 1)

            pe.wait_ge(a_free, A_LOGITS + 1)
            pe.wait_ge(xT_kept, B)
            shared_up(0)
            shared_down(0)
            shared_up(1)
            pe.wait_ge(sel_ready, 1)
            pe.wait_ge(s_yfree, 2)
            rank = Bk[:, 2, 0:TE].rearrange("p (t e) -> p t e", e=E)
            mm(rank, beforeb[:], selb, start=True, stop=False, skip_group_check=True)
            for s in range(1, T):
                mm(rank[:, s:T, :], onesb[:], selb[:, 0:T - s, :], start=False, stop=s == T - 1,
                   skip_group_check=True)
            for t in range(T):
                last = mm(Bk[:, 3, 0:E], onesb[:], selb[:, t, :], start=t == 0, stop=t == T - 1)
            last.then_inc(rank_full, 1)
            pe.wait_ge(slots_ready, TOP_K)
            shared_down(1)
            with pe.Fori(2, B) as b:
                shared_up(b)
                shared_down(b)

            def rows_t(t, a):
                pe.wait_ge(e_in[a], DMA * (t // 2 + 1) if isinstance(t, int) else DMA * half(t, a))
                for c in range(C):
                    last = tr(Bk[:, 0, c * P:(c + 1) * P], e_x[:, a, c * P:(c + 1) * P], ident[:])
                last.then_inc(e_xt, 1)

            def up(t, a):
                e = pe.value_load(expert_of[0:1, bass.ds(t, 1)], min_val=0, max_val=E - 1)
                pe.wait_ge(e_xTr, t + 1)
                for i in range(2):
                    for c in range(C):
                        last = mm(A[:, 2 * a + i, 0:HALF], e_xT[:, a, c, :],
                                  wup[:, c, bass.ds(e * (2 * HALF) + i * HALF, HALF)],
                                  start=c == 0, stop=c == C - 1)
                last.then_inc(e_up, 1)
                return e

            def down(t, a, e):
                pe.wait_ge(e_hr, t + 1)
                for m in range(M):
                    last = tr(Bk[:, 1, m * P:(m + 1) * P], e_h[:, a, m * P:(m + 1) * P], ident[:])
                last.then_inc(e_ht, 1)
                pe.wait_ge(e_hTr, t + 1)
                pe.wait_ge(e_yr, t + 1)
                for m in range(M):
                    last = mm(Bk[:, 2, 0:D], e_hT[:, a, m, :], wdn[:, m, bass.ds(e * D, D)],
                              start=m == 0, stop=m == M - 1)
                last.then_inc(e_yf, 1)

            def expert(t):
                return pe.value_load(expert_of[0:1, bass.ds(t, 1)], min_val=0, max_val=E - 1)

            def half(t, a):
                return (t - a) // 2 + 1

            pe.wait_ge(s_yfree, B + 1)
            rows_t(0, 0)
            up(0, 0)
            with pe.Fori(0, NT // 2 - 1) as i:
                t = 2 * i
                pe.wait_ge(e_in[1], DMA * (i + 1))
                for c in range(C):
                    last = tr(Bk[:, 0, c * P:(c + 1) * P], e_x[:, 1, c * P:(c + 1) * P], ident[:])
                last.then_inc(e_xt, 1)
                up(t + 1, 1)
                down(t, 0, expert(t))
                pe.wait_ge(e_in[0], DMA * (i + 2))
                for c in range(C):
                    last = tr(Bk[:, 0, c * P:(c + 1) * P], e_x[:, 0, c * P:(c + 1) * P], ident[:])
                last.then_inc(e_xt, 1)
                up(t + 2, 0)
                down(t + 1, 1, expert(t + 1))
            rows_t(NT - 1, 1)
            up(NT - 1, 1)
            down(NT - 2, 0, expert(NT - 2))
            down(NT - 1, 1, expert(NT - 1))

        @block.scalar
        def _(act):
            copy = lambda o, i: nc.scalar.activation(o, i, ACT.Copy)

            act.wait_ge(ln_step, 5)
            nc.scalar.activation(std[:], st_a[:], ACT.Sqrt).then_inc(std_ready, 1)
            act.wait_ge(std_ready, 1)
            copy(st_b[:], std[:]).then_inc(b_free, 1)
            with act.Fori(0, B) as b:
                act.wait_ge(b_full, b + 1)
                copy(xnT[:, :, bass.ds(b * S, S)], Bk[:, 0:C, :]).then_inc(b_free, 1)

            def batch(b):
                n = B_ATT + b * B_PER
                for g in range(NG):
                    for k in range(QT):
                        act.wait_ge(b_full, n + k + 1)
                        nc.scalar.activation(pT[k], Bk[:, :, 0:S - k * P], ACT.Exp).then_inc(b_free, 1)
                    act.wait_ge(b_full, n + QT + 1)
                    copy(oT[:, g, :], Bk[:, 0, :]).then_inc(b_free, 1)
                    n = n + QT + 1
                act.wait_ge(b_full, n + 1)
                copy(attnT, Bk[:, 0:C, :]).then_inc(b_free, 1)

            with act.Fori(0, B) as b:
                batch(b)

            act.wait_ge(ln_step, 10)
            nc.scalar.activation(std[:], st_a[:], ACT.Sqrt).then_inc(std_ready, 1)
            with act.Fori(0, B) as b:
                act.wait_ge(b_full, B_LN2 + b + 1)
                copy(xTs, Bk[:, 0:C, :]).then_inc(b_free, 1)

            act.wait_ge(d_ready, 1)
            nc.scalar.activation(ex, dl, ACT.Exp).then_inc(ex_ready, 1)
            gate = [A[:, 0, :], A[:, 2, :], Bk[:, 0, :]]
            with act.Fori(0, B) as b:
                for m in range(M):
                    act.wait_ge(s_up, b * M + m + 1)
                    nc.scalar.activation(sg[:, m, :], gate[m], ACT.Silu).then_inc(s_sg, 1)

            def front(t, a):
                act.wait_ge(e_xt, t + 1)
                copy(e_xT[:, a], Bk[:, 0, 0:C * P].rearrange("p (c n) -> p c n", c=C)).then_inc(e_xTr, 1)
                act.wait_ge(e_up, t + 1)
                nc.scalar.activation(e_sg[:, a, :], A[:, 2 * a, 0:HALF], ACT.Silu).then_inc(e_sgr, 1)

            def back(t, a):
                act.wait_ge(e_ht, t + 1)
                copy(e_hT[:, a], Bk[:, 1, 0:M * P].rearrange("p (c n) -> p c n", c=M)).then_inc(e_hTr, 1)

            front(0, 0)
            with act.Fori(0, NT // 2 - 1) as i:
                front(2 * i + 1, 1)
                back(2 * i, 0)
                front(2 * i + 2, 0)
                back(2 * i + 1, 1)
            front(NT - 1, 1)
            back(NT - 2, 0)
            back(NT - 1, 1)

        @block.vector
        def _(dve):
            v = nc.vector

            def moments(first):
                me, mo, qe, qo = (stats[:, :, k] for k in (1, 4, 2, 5))
                dve.wait_ge(st_done, T * (1 if first else 2))
                base = 0 if first else 5
                v.tensor_tensor(mean[:], me, mo, ALU.add).then_inc(ln_step, 1)
                v.tensor_tensor(st_c[:], qe, qo, ALU.add).then_inc(ln_step, 1)
                v.tensor_tensor(st_a[:], me, mo, ALU.subtract).then_inc(ln_step, 1)
                dve.wait_ge(ln_step, base + 3)
                v.scalar_tensor_tensor(out=st_a[:], in0=st_a[:], scalar=0.25, in1=st_a[:], op0=ALU.mult,
                                       op1=ALU.mult).then_inc(ln_step, 1)
                v.tensor_scalar(mean[:], mean[:], 0.5, None, ALU.mult).then_inc(mean_done, 1)
                v.tensor_scalar(st_c[:], st_c[:], 1.0 / D, EPS, ALU.mult, ALU.add).then_inc(mean_done, 1)
                dve.wait_ge(ln_step, base + 4)
                dve.wait_ge(mean_done, 2 if first else 5)
                v.tensor_tensor(st_a[:], st_a[:], st_c[:], ALU.add).then_inc(ln_step, 1)
                dve.wait_ge(std_ready, 1 if first else 2)
                v.reciprocal(rstd[:], std[:]).then_inc(mean_done, 1)
                dve.wait_ge(mean_done, 3 if first else 6)

            def normalised(b, dst):
                for j in range(QT):
                    t = b * QT + j
                    last = v.tensor_scalar(dst(j), xs_all[:, bass.ds(t, 1), :], mean[:, bass.ds(t, 1)],
                                           rstd[:, bass.ds(t, 1)], ALU.subtract, ALU.mult)
                return last

            for b in range(B):
                dve.wait_ge(ld_x[b], DMA)
                for j in range(QT):
                    v.bn_stats(stats[:, b * QT + j, :], xs_all[:, b * QT + j, :]).then_inc(st_done, 1)
            moments(True)
            normalised(0, lambda j: xs[:, j:j + 1, :]).then_inc(xs_ready, 1)
            with dve.Fori(1, B) as b:
                dve.wait_ge(b_full, b)
                normalised(b, lambda j: xs[:, j:j + 1, :]).then_inc(xs_ready, 1)

            dve.wait_ge(consts, 1)
            dve.wait_ge(pads_set, DMA * 2 * HG)
            v.reduce_sum(ones_row, ident[:, DK:P:32], AX.X).then_inc(pads_dve, 1)
            dve.wait_ge(pads_dve, 1)
            v.tensor_scalar(bkc, bkc, ones_row, None, ALU.add).then_inc(pads_dve, 1)
            dve.wait_ge(pads_dve, 2)

            def qk(g, n):
                dve.wait_ge(a_full, n + 1)
                v.tensor_scalar(qT, A[:, 0, :], bqc[:, g:g + 1], SCALE, ALU.add, ALU.mult).then_inc(q_kept, 1)
                v.tensor_scalar(kT[:, g % 2, :], A[:, 1, :], bkc[:, g:g + 1], None, ALU.add).then_inc(a_free, 1)

            def rowmax(k, n):
                dve.wait_ge(a_full, n + 1)
                v.tensor_reduce(mz[:, k, DK:P:32], A[:, :, 0:(k + 1) * P], AX.X, ALU.max,
                                negate=True).then_inc(a_free, 1)

            def maxima(g, n):
                dve.wait_ge(a_full, n + 1)
                v.tensor_tensor(qaT[:, g % 2, :], qT, A[:, 0, :], ALU.add).then_inc(a_free, 1)

            qk(0, 0)
            for k in range(QT):
                rowmax(k, 1 + k)
            maxima(0, QT + 1)

            def batch(b, final):
                n = A_PRO + b * A_PER
                dve.wait_ge(a_full, n + 1)
                vv = A[:, 0:2, :].rearrange("p a (k h i) -> p (a k) h i", k=2, h=H)
                bb = bv_bc.rearrange("p (o h i) -> p o h i", o=1, h=H).to_broadcast([P, QT, H, DK])
                v.tensor_tensor(vaug[:, :, :, 0:DK], vv, bb, ALU.add).then_inc(a_free, 1)
                n = n + 1
                for s in range(NG):
                    if final and s == NG - 1:
                        break
                    g1 = (s + 1) % NG
                    qk(g1, n)
                    for k in range(QT):
                        rowmax(QT - 1 - k, n + 1 + k)
                    maxima(g1, n + QT + 1)
                    n = n + QT + 2
                dve.wait_ge(a_full, n + 1)
                o = A[:].rearrange("p k (h w) -> p k h w", w=32)
                v.reciprocal(rc, o[:, :, :, DK]).then_inc(rc_ready, 1)
                dve.wait_ge(rc_ready, b + 1)
                v.tensor_tensor(attn.rearrange("p k (h i) -> p k h i", h=H), o[:, :, :, 0:DK],
                                rc.rearrange("p k (h o) -> p k h o", o=1).to_broadcast([P, QT, H, DK]),
                                ALU.mult).then_inc(a_free, 1)
                dve.wait_ge(a_full, n + 2)
                rows = xs_all[:, bass.ds(b * QT, QT), :]
                v.tensor_tensor(rows, A[:, 0:2, :].rearrange("p a (k d) -> p (a k) d", k=2), rows,
                                ALU.add).then_inc(a_free, 1)

            dve.wait_ge(bo_added, 1)
            with dve.Fori(0, B - 1) as b:
                batch(b, False)
            batch(B - 1, True)

            dve.wait_ge(a_free, A_LOGITS)
            for t in range(T):
                v.bn_stats(stats[:, t, :], xs_all[:, t, :]).then_inc(st_done, 1)
            moments(False)
            normalised(0, lambda j: xs2[:, j:j + 1, :]).then_inc(xs_ready, 1)
            normalised(0, lambda j: xn2[:, j:j + 1, :]).then_inc(kept, 1)
            dve.wait_ge(b_full, B_LN2 + 1)
            with dve.Fori(1, B) as b:
                dve.wait_ge(b_full, B_LN2 + b)
                dve.wait_ge(b_free, B_LN2 + b + 1)
                v.tensor_copy(xn2T[:, :, bass.ds((b - 1) * S, S)], xTs).then_inc(xT_kept, 1)
                dve.wait_ge(xT_kept, b)
                normalised(b, lambda j: xs2[:, j:j + 1, :]).then_inc(xs_ready, 1)
                normalised(b, lambda j: xn2[:, bass.ds(b * QT + j, 1), :]).then_inc(kept, 1)
            dve.wait_ge(b_free, B_LN2 + B + 1)
            v.tensor_copy(xn2T[:, :, (B - 1) * S:B * S], xTs).then_inc(xT_kept, 1)

            steps = [0]

            def link(ins):
                steps[0] += 1
                ins.then_inc(route, 1)
                dve.wait_ge(route, steps[0])

            def over_e(col):
                return col.rearrange("p (t o) -> p t o", o=1).to_broadcast([P, T, E])

            dve.wait_ge(a_full, A_LOGITS + B)
            dve.wait_ge(rconsts, 6)
            v.tensor_copy(lg, A[:, 0, 0:TE].rearrange("p (t e) -> p t e", e=E)).then_inc(a_free, 1)

            def shared_h(b):
                for m in range(M):
                    dve.wait_ge(s_sg, b * M + m + 1)
                    up_ = (A[:, 1, :], A[:, 3, :], Bk[:, 1, :])[m]
                    v.tensor_tensor(hT[:, m, :], up_, sg[:, m, :], ALU.mult).then_inc(s_h, 1)

            def shared_y(b):
                dve.wait_ge(s_y, b + 1)
                rows = xs_all[:, bass.ds(b * QT, QT), :]
                v.tensor_tensor(rows, Bk[:, 2:4, :].rearrange("p a (k d) -> p (a k) d", k=2), rows,
                                ALU.add).then_inc(s_yfree, 1)

            dve.wait_ge(a_free, A_LOGITS + 1)
            link(v.tensor_reduce(m1, lg, AX.X, ALU.max))
            link(v.tensor_tensor(ra, lg, over_e(m1), ALU.is_equal))
            link(v.scalar_tensor_tensor(out=ra, in0=ra, scalar=-float(E), in1=io8, op0=ALU.mult, op1=ALU.add))
            link(v.tensor_reduce(i1, ra, AX.X, ALU.min))
            link(v.tensor_tensor(oh1, io, over_e(i1), ALU.is_equal))
            link(v.scalar_tensor_tensor(out=rb, in0=oh1, scalar=LOWEST, in1=lg, op0=ALU.mult, op1=ALU.add))
            link(v.tensor_reduce(m2, rb, AX.X, ALU.max))
            link(v.tensor_tensor(ra, rb, over_e(m2), ALU.is_equal))
            link(v.scalar_tensor_tensor(out=ra, in0=ra, scalar=-float(E), in1=io8, op0=ALU.mult, op1=ALU.add))
            link(v.tensor_reduce(i2, ra, AX.X, ALU.min))
            link(v.tensor_tensor(oh2, io, over_e(i2), ALU.is_equal))
            v.tensor_tensor(dl, m2, m1, ALU.subtract).then_inc(d_ready, 1)
            v.tensor_tensor(selb, oh1, oh2, ALU.add).then_inc(sel_ready, 1)
            dve.wait_ge(ex_ready, 1)
            link(v.tensor_scalar(sm, ex, 1.0, None, ALU.add))
            link(v.reciprocal(wts[:, 0, :], sm))
            link(v.tensor_tensor(wts[:, 1, :], ex, wts[:, 0, :], ALU.mult))
            dve.wait_ge(kept, B)
            shared_h(0)
            shared_y(0)

            dve.wait_ge(rank_full, 1)
            link(v.tensor_copy(tot, Bk[:, 3, 0:E]))
            link(v.tensor_tensor(k128, tot.rearrange("p (e o) -> p e o", o=1).to_broadcast([P, E, T]), k128,
                                 ALU.is_gt))
            link(v.tensor_reduce(tiles_of, k128, AX.X, ALU.add))
            link(v.tensor_tensor(ee, tiles_of.rearrange("p (o e) -> p o e", o=1).to_broadcast([P, E, E]), upto,
                                 ALU.mult))
            link(v.tensor_reduce(ends, ee, AX.X, ALU.add))
            link(v.tensor_tensor(base, ends, tiles_of, ALU.subtract))
            link(v.scalar_tensor_tensor(
                out=rslot, in0=base.rearrange("p (o e) -> p o e", o=1).to_broadcast([P, T, E]), scalar=float(P),
                in1=Bk[:, 2, 0:TE].rearrange("p (t e) -> p t e", e=E), op0=ALU.mult, op1=ALU.add))
            link(v.tensor_tensor(tcmp, ends.rearrange("p (o e) -> p o e", o=1).to_broadcast([P, NT, E]), tio,
                                 ALU.is_le))
            link(v.tensor_reduce(tnum, tcmp, AX.X, ALU.add))
            v.tensor_scalar(expert_of[:], tnum, float(E - 1), None, ALU.min).then_inc(kept, 1)
            for k, oh in enumerate((oh1, oh2)):
                link(v.tensor_tensor(oh, oh, rslot, ALU.mult))
                link(v.tensor_reduce(slotf[:, k, :], oh, AX.X, ALU.add))
                v.tensor_copy(slots[:, k, :], slotf[:, k, :]).then_inc(slots_ready, 1)

            with dve.Fori(1, B) as b:
                shared_h(b)
                shared_y(b)

            def hidden(t, a):
                dve.wait_ge(e_sgr, t + 1)
                v.tensor_tensor(e_h[:, a, :], A[:, 2 * a + 1, 0:HALF], e_sg[:, a, :], ALU.mult).then_inc(e_hr, 1)

            def result(t, a, i):
                dve.wait_ge(e_yf, t + 1)
                dve.wait_ge(e_out[a], DMA * (i + 1))
                v.tensor_copy(e_y[:, a, :], Bk[:, 2, 0:D]).then_inc(e_yr, 1)

            hidden(0, 0)
            with dve.Fori(0, NT // 2 - 1) as i:
                hidden(2 * i + 1, 1)
                result(2 * i, 0, i)
                hidden(2 * i + 2, 0)
                result(2 * i + 1, 1, i)
            hidden(NT - 1, 1)
            result(NT - 2, 0, NT // 2 - 1)
            result(NT - 1, 1, NT // 2 - 1)

            for t in range(T):
                dve.wait_ge(y_in[t % NYB], DMA * TOP_K * (t // NYB + 1))
                row = xs_all[:, t, :]
                v.scalar_tensor_tensor(out=row, in0=yb[:, t % NYB, 0, :], scalar=wts[:, 0, t:t + 1], in1=row,
                                       op0=ALU.mult, op1=ALU.add).then_inc(comb1, 1)
                dve.wait_ge(comb1, t + 1)
                v.scalar_tensor_tensor(out=row, in0=yb[:, t % NYB, 1, :], scalar=wts[:, 1, t:t + 1], in1=row,
                                       op0=ALU.mult, op1=ALU.add).then_inc(comb2, 1)


def kernel(x, ctx_1024, L0_xattn_Wq, L0_xattn_bq, L0_xattn_Wk, L0_xattn_bk, L0_xattn_Wv, L0_xattn_bv,
           L0_xattn_Wo, L0_xattn_bo, L0_ffn_gate_w, L0_ffn_w_up, L0_ffn_w_down, L0_ffn_sg_gate,
           L0_ffn_sg_up, L0_ffn_sg_down):
    import numpy as np
    import concourse.bacc as bacc
    from concourse.bass_utils import run_bass_kernel_spmd

    def by_head(bias):
        return np.transpose(np.reshape(bias, (NUM_HEADS // 4, 4, -1)), (1, 2, 0))

    arrays = {
        "x": x,
        "ctxT": np.transpose(ctx_1024, (0, 2, 1)),
        "wqT": np.transpose(L0_xattn_Wq), "bq": by_head(L0_xattn_bq),
        "wkT": np.transpose(L0_xattn_Wk), "bk": by_head(L0_xattn_bk),
        "wvT": np.transpose(L0_xattn_Wv), "bv": L0_xattn_bv,
        "woT": np.transpose(L0_xattn_Wo), "bo": L0_xattn_bo,
        "gwT": np.transpose(L0_ffn_gate_w),
        "wupT": np.transpose(L0_ffn_w_up, (2, 0, 1)).reshape(L0_ffn_w_up.shape[2], -1),
        "wdnT": np.transpose(L0_ffn_w_down, (2, 0, 1)).reshape(L0_ffn_w_down.shape[2], -1),
        "sgT": np.transpose(L0_ffn_sg_gate),
        "suT": np.transpose(L0_ffn_sg_up),
        "sdT": np.transpose(L0_ffn_sg_down),
    }
    arrays = {k: np.ascontiguousarray(v) for k, v in arrays.items()}
    nc = bacc.Bacc("TRN2", target_bir_lowering=False, num_devices=1)
    aps = {k: nc.dram_tensor(f"in_{k}", a.shape, mybir.dt.from_np(a.dtype), kind="ExternalInput").ap()
           for k, a in arrays.items()}
    out = nc.dram_tensor("out", x.shape, mybir.dt.from_np(np.dtype(x.dtype)), kind="ExternalOutput").ap()
    build(nc, *aps.values(), out)
    r = run_bass_kernel_spmd(nc, [{f"in_{k}": a for k, a in arrays.items()}], core_ids=[0])
    return r.results[0]["out"]
```

```python
from contextlib import ExitStack

import concourse.bass as bass
from concourse import mybir

P = 128
F32 = mybir.dt.float32
BF16 = mybir.dt.bfloat16
I32 = mybir.dt.int32
ALU = mybir.AluOpType
ACT = mybir.ActivationFunctionType
AX = mybir.AxisListType

NUM_HEADS = 16
EPS = 1e-5
MASKED = -1e30
LOWEST = -3e38
DMA = 16


def build(nc, x, ctxT, wqT, bq, wkT, bk, wvT, bv, woT, bo, gwT, wupT, wdnT, sgT, suT, sdT, out):
    B, S, D = x.shape
    H = NUM_HEADS
    DK = D // H
    HG = P // 32
    NG = H // HG
    HH = P // DK
    C = D // P
    QT = S // P
    N = B * S
    T = N // P
    E = gwT.shape[1]
    HALF = sgT.shape[1]
    M = HALF // P
    TOP_K = 2
    NT = (TOP_K * N + E * (P - 1)) // P
    NT += 1 - NT % 2
    SCALE = float(DK) ** -0.5
    Q_PART = (0, 0, 1, 1, 0, 2)
    K_PART = (0, 1, 0, 1, 2, 0)
    ROWS = DK * len(Q_PART)
    assert S == 512 and D == 256 and H == 2 * HH and ROWS == 96

    with ExitStack() as ctx:
        def sb(name, shape, dt=F32):
            return ctx.enter_context(nc.sbuf_tensor(name, shape, dt))

        def sem(name):
            return ctx.enter_context(nc.semaphore(name))

        xg = nc.dram_tensor("x_by_slot", (NT * P, D), F32, kind="Internal").ap()
        yg = nc.dram_tensor("y_by_slot", (NT * P, D), F32, kind="Internal").ap()

        A = ctx.enter_context(nc.psum_tensor("set_a", [P, 4, 512], F32))
        Bk = ctx.enter_context(nc.psum_tensor("set_b", [P, 4, 512], F32))

        xs_all = sb("x_res", [P, T, D])
        wdn = sb("w_down", [P, M, E * D])
        wsg = sb("w_sg", [P, C, HALF])
        wsu = sb("w_su", [P, C, HALF])
        wsd = sb("w_sd", [P, M, D])
        gw = sb("gate_w", [P, C, E])
        ident = sb("ident", [P, P])
        identb = sb("identb", [P, P], BF16)
        maskb = sb("maskb", [P, P], BF16)
        beforeb = sb("beforeb", [P, P], BF16)
        onesb = sb("onesb", [P, P], BF16)
        slots = sb("slots", [P, TOP_K, T], I32)
        wts = sb("wts", [P, TOP_K, T])
        expert_of = sb("expert_of", [P, NT], I32)
        stats = sb("stats", [P, T, 6])
        st_a = sb("st_a", [P, T])
        st_b = sb("st_b", [P, T])
        st_c = sb("st_c", [P, T])
        mean = sb("mean", [P, T])
        rstd = sb("rstd", [P, T])
        std = sb("std", [P, T])

        credit = sb("credit", [P, 4])

        KB = 256
        REGION = 140 * KB
        region = sb("region", [P, REGION])
        used = [0]

        def part(words, restart=False):
            if restart:
                used[0] = 0
            lo = used[0]
            used[0] += words
            assert used[0] <= REGION, used[0] / KB
            return region[:, lo:lo + words]

        xnT = part(C * N).rearrange("p (c n) -> p c n", c=C)
        cT = part(C * N).rearrange("p (c n) -> p c n", c=C)
        pT_at = [sum(HG * (S - P * j) for j in range(k)) for k in range(QT + 1)]
        pT_all = part(pT_at[QT])
        pT = [pT_all[:, pT_at[k]:pT_at[k + 1]].rearrange("p (h q) -> p h q", h=HG) for k in range(QT)]
        qstack = part(2 * HH * S // 2).bitcast(BF16).rearrange("p (a h n) -> p a h n", a=2, h=HH)
        kstack = part(2 * HH * S // 2).bitcast(BF16).rearrange("p (a h n) -> p a h n", a=2, h=HH)
        val = part(2 * S).rearrange("p (a n) -> p a n", a=2)
        rem = part(2 * S).rearrange("p (a n) -> p a n", a=2)
        parts = part(2 * 3 * S // 2).bitcast(BF16).rearrange("p (a i n) -> p a i n", a=2, i=3)
        mneg = part(QT * HG).rearrange("p (k h) -> p k h", k=QT)
        mrem = part(QT * HG).rearrange("p (k h) -> p k h", k=QT)
        mparts = part(QT * 3 * HG // 2).bitcast(BF16).rearrange("p (k i h) -> p k i h", k=QT, i=3)
        mrows = part(S // 2).bitcast(BF16)
        vaug = part(QT * H * 32).rearrange("p (k h w) -> p k h w", k=QT, h=H)
        oT = part(NG * S).rearrange("p (g n) -> p g n", g=NG)
        attn = part(QT * D).rearrange("p (k d) -> p k d", k=QT)
        attnT = part(C * S).rearrange("p (c n) -> p c n", c=C)
        cV = part(C * S).rearrange("p (c n) -> p c n", c=C)
        wq = part(C * D).rearrange("p (c n) -> p c n", c=C)
        wk = part(C * D).rearrange("p (c n) -> p c n", c=C)
        wv = part(C * D).rearrange("p (c n) -> p c n", c=C)
        wo = part(C * D).rearrange("p (c n) -> p c n", c=C)
        bv_bc = part(D)
        bo_bc = part(D)
        rc = part(QT * H).rearrange("p (k h) -> p k h", k=QT)
        bqc = part(2)
        bkc = part(2)
        xs = [attn, attnT.rearrange("p c (k d) -> p (c k) d", d=D)]
        zeros = oT[:, 3, 0:D]

        xn2 = part(T * D, restart=True).rearrange("p (t d) -> p t d", t=T)
        xn2T = part(C * N).rearrange("p (c n) -> p c n", c=C)
        wup = part(C * E * 2 * HALF).rearrange("p (c n) -> p c n", c=C)
        sg = part(M * S).rearrange("p (m n) -> p m n", m=M)
        hT = part(M * S).rearrange("p (m n) -> p m n", m=M)
        TE = T * E

        def te():
            return part(TE).rearrange("p (t e) -> p t e", e=E)

        lg, io, io8, oh1, oh2, ra, rb, rslot = (te() for _ in range(8))
        selb = part(TE // 2).bitcast(BF16).rearrange("p (t e) -> p t e", e=E)
        m1, m2, i1, i2, dl, ex, sm = (part(T) for _ in range(7))
        k128 = part(E * T).rearrange("p (e k) -> p e k", e=E)
        upto = part(E * E).rearrange("p (a b) -> p a b", a=E)
        tot, tiles_of, ends, base = (part(E) for _ in range(4))
        ee = part(E * E).rearrange("p (a b) -> p a b", a=E)
        tio = part(NT * E).rearrange("p (t e) -> p t e", e=E)
        tcmp = part(NT * E).rearrange("p (t e) -> p t e", e=E)
        tnum = part(NT)
        slotf = part(TOP_K * T).rearrange("p (k t) -> p k t", k=TOP_K)
        e_x = part(2 * D).rearrange("p (a d) -> p a d", a=2)
        e_xT = part(2 * C * P).rearrange("p (a c n) -> p a c n", a=2, c=C)
        e_sg = part(2 * HALF).rearrange("p (a d) -> p a d", a=2)
        e_h = part(2 * HALF).rearrange("p (a d) -> p a d", a=2)
        e_hT = part(2 * M * P).rearrange("p (a c n) -> p a c n", a=2, c=M)
        e_y = part(2 * D).rearrange("p (a d) -> p a d", a=2)
        NYB = 4
        yb = part(NYB * TOP_K * D).rearrange("p (a k d) -> p a k d", a=NYB, k=TOP_K)

        ld_x = [sem(f"ld_x{b}") for b in range(B)]
        ld_qk, ld_ctx0, ld_ctx, ld_wvo, ld_cv, ld_moe, ld_up = (sem(n) for n in
            ("ld_qk", "ld_ctx0", "ld_ctx", "ld_wvo", "ld_cv", "ld_moe", "ld_up"))
        zero_ready, xg_zeroed = sem("zero_ready"), sem("xg_zeroed")
        consts, pads, fills = sem("consts"), sem("pads"), sem("fills")
        st_done, ln_step, std_ready, xs_ready = sem("st_done"), sem("ln_step"), sem("std_ready"), sem("xs_ready")
        mean_done, kept, xnT_ready = sem("mean_done"), sem("kept"), sem("xnT_ready")
        val_ready, part1_ready, rem_ready, part2_ready, parts_ready = (sem(n) for n in
            ("val_ready", "part1_ready", "rem_ready", "part2_ready", "parts_ready"))
        rows_in = [sem("rows_in0"), sem("rows_in1")]
        max_ready, mpart_step, mparts_ready, max_in = (sem(n) for n in
            ("max_ready", "mpart_step", "mparts_ready", "max_in"))
        bo_added = sem("bo_added")
        a_full, a_free, b_full, b_free = sem("a_full"), sem("a_free"), sem("b_full"), sem("b_free")
        p_masked, rc_ready, mask_turn = sem("p_masked"), sem("rc_ready"), sem("mask_turn")
        xT_kept, route, d_ready, ex_ready, sel_ready, rank_full, slots_ready = (sem(n) for n in
            ("xT_kept", "route", "d_ready", "ex_ready", "sel_ready", "rank_full", "slots_ready"))
        rconsts, scattered = sem("rconsts"), sem("scattered")
        s_up, s_sg, s_h, s_y, s_yfree = (sem(n) for n in ("s_up", "s_sg", "s_h", "s_y", "s_yfree"))
        e_in = [sem("e_in0"), sem("e_in1")]
        e_out = [sem("e_out0"), sem("e_out1")]
        e_xt, e_xTr, e_up, e_sgr, e_hr, e_ht, e_hTr, e_yf, e_yr = (sem(n) for n in
            ("e_xt", "e_xTr", "e_up", "e_sgr", "e_hr", "e_ht", "e_hTr", "e_yf", "e_yr"))
        y_in = [sem(f"y_in{i}") for i in range(NYB)]
        comb1, comb2, stored = sem("comb1"), sem("comb2"), sem("stored")

        HP = HG // 2
        A_GRP = HP * QT
        A_PRO = 3 + A_GRP
        A_PER = 2 + 1 + NG * A_GRP + 2 + 1
        A_END = 1 + NG * A_GRP
        A_LOGITS = A_PRO + B * A_PER - 3 - A_GRP
        LEAD = 4
        B_GRP = HP * QT + 2
        B_PER = NG * B_GRP + 2
        B_ATT = B + 1
        B_LN2 = B_ATT + B * B_PER - 1
        assert A_PER % 2 == 0 and B_PER % 2 == 0

        def pair(bank_set, n):
            return bank_set[:, n % 2 * 2:n % 2 * 2 + 2, :]

        block = ctx.enter_context(nc.Block())

        @block.sync
        def _(sp):
            x_t = x.rearrange("b (k p) d -> b p k d", p=P)
            for b in range(B):
                sp.dma_start(xs_all[:, b * QT:(b + 1) * QT, :], x_t[b]).then_inc(ld_x[b], DMA)
            for w, w_dram in ((wq, wqT), (wk, wkT)):
                sp.dma_start(w, w_dram.rearrange("(c p) n -> p c n", p=P)).then_inc(ld_qk, DMA)
            sp.dma_start(bqc, bq).then_inc(ld_qk, DMA)
            sp.dma_start(bkc, bk).then_inc(ld_qk, DMA)
            for b in range(B):
                sp.dma_start(cT[:, :, b * S:(b + 1) * S],
                             ctxT[b].rearrange("(c p) n -> p c n", p=P)[:, :, 0:S]
                             ).then_inc(ld_ctx if b else ld_ctx0, DMA)
            sp.dma_start(wv, wvT.rearrange("(c p) n -> p c n", p=P)).then_inc(ld_wvo, DMA)
            sp.dma_start(wo, woT.rearrange("(c p) n -> p c n", p=P)).then_inc(ld_wvo, DMA)
            sp.dma_start(bv_bc, bv.partition_broadcast(P)).then_inc(ld_wvo, DMA)
            sp.dma_start(bo_bc, bo.partition_broadcast(P)).then_inc(ld_wvo, DMA)
            sp.dma_start(cV, ctxT[0].rearrange("(c p) n -> p c n", p=P)[:, :, 0:S]).then_inc(ld_cv, DMA)

            def stack(half, u):
                for a, (dst, order) in enumerate(((qstack, Q_PART), (kstack, K_PART))):
                    sp.wait_ge(parts_ready, 2 * u + a + 1)
                    for j, part_of in enumerate(order):
                        sp.dma_start(dst[DK * j:DK * (j + 1), half, :, :],
                                     parts[:, a, part_of, :]).then_inc(rows_in[half], DMA)

            def max_rows(g, n):
                sp.wait_ge(b_free, n + 1)
                h = g % 2 * HG
                sp.dma_start(qstack[ROWS:ROWS + 3, g // 2, h:h + HG, :], mrows[0:3 * HG, :]).then_inc(max_in, DMA)

            stack(0, 0)
            sp.wait_ge(fills, 2)
            sp.dma_start(xg.rearrange("(t p) d -> p t d", p=P),
                         zeros.rearrange("p (o d) -> p o d", o=1).to_broadcast([P, NT, D])).then_inc(xg_zeroed, DMA)
            sp.dma_start(wsg[:], sgT.rearrange("(c p) n -> p c n", p=P)).then_inc(ld_moe, DMA)
            sp.dma_start(wsu[:], suT.rearrange("(c p) n -> p c n", p=P)).then_inc(ld_moe, DMA)
            sp.dma_start(wsd[:], sdT.rearrange("(c p) n -> p c n", p=P)).then_inc(ld_moe, DMA)
            sp.dma_start(gw[:], gwT.rearrange("(c p) n -> p c n", p=P)).then_inc(ld_moe, DMA)
            max_rows(0, B_ATT - 1)
            for m in range(M):
                sp.dma_start(wdn[:, m, :], wdnT[m * P:(m + 1) * P]).then_inc(ld_moe, DMA)

            def batch(b, final):
                n_b = B_ATT + b * B_PER
                stack(1, 2 * b + 1)
                if not final:
                    sp.wait_ge(a_full, A_PRO + b * A_PER - 1)
                    sp.dma_start(cV, ctxT[bass.ds(b + 1, 1)].rearrange("o (c p) n -> p (o c) n", p=P)[:, :, 0:S]
                                 ).then_inc(ld_cv, DMA)
                max_rows(1, n_b + A_GRP)
                max_rows(2, n_b + B_GRP + A_GRP)
                if not final:
                    sp.wait_ge(b_full, n_b + B_GRP + A_GRP)
                    stack(0, 2 * b + 2)
                max_rows(3, n_b + 2 * B_GRP + A_GRP)
                if not final:
                    max_rows(0, n_b + 3 * B_GRP + A_GRP)

            with sp.Fori(0, B - 1) as b:
                batch(b, False)
            batch(B - 1, True)
            sp.wait_ge(a_free, A_LOGITS)
            for c in range(C):
                sp.dma_start(wup[:, c, :], wupT[c * P:(c + 1) * P]).then_inc(ld_up, DMA)

            xg_t = xg.rearrange("(t p) d -> t p d", p=P)
            yg_t = yg.rearrange("(t p) d -> t p d", p=P)
            sp.wait_ge(scattered, DMA * TOP_K * T)
            for a in range(2):
                sp.dma_start(e_x[:, a, :], xg_t[a]).then_inc(e_in[a], DMA)
            for t in range(2, 5):
                sp.wait_ge(e_xt, t - 1)
                sp.dma_start(e_x[:, t % 2, :], xg_t[t]).then_inc(e_in[t % 2], DMA)
            with sp.Fori(0, (NT - 5) // 2) as i:
                for a in (1, 0):
                    t = 2 * i + (1 if a else 2)
                    sp.wait_ge(e_xt, t + 3)
                    sp.dma_start(e_x[:, a, :], xg[bass.ds((t + 4) * P, P), :]).then_inc(e_in[a], DMA)
                    sp.wait_ge(e_yr, t + 1)
                    sp.dma_start(yg[bass.ds((t - 1) * P, P), :], e_y[:, 1 - a, :]).then_inc(e_out[1 - a], DMA)
            for t in range(NT - 5, NT):
                sp.wait_ge(e_yr, t + 2)
                sp.dma_start(yg_t[t], e_y[:, t % 2, :]).then_inc(e_out[t % 2], DMA)

            o_t = out.rearrange("b (k p) d -> (b k) p d", p=P)
            for t in range(T):
                sp.wait_ge(comb2, t + 1)
                sp.dma_start(o_t[t], xs_all[:, t, :]).then_inc(stored, DMA)
            sp.wait_ge(stored, DMA * T)

        @block.gpsimd
        def _(pool):
            g = nc.gpsimd
            g.memset(ident[:], 0.0).then_inc(pads, 1)
            pool.wait_ge(pads, 1)
            g.affine_select(out=ident[:], in_=ident[:], compare_op=ALU.not_equal, fill=1.0, base=0,
                            pattern=[[-1, P]], channel_multiplier=1).then_inc(consts, 1)
            g.memset(identb[:], 0.0).then_inc(pads, 1)
            g.memset(maskb[:], 0.0).then_inc(pads, 1)
            g.memset(beforeb[:], 0.0).then_inc(pads, 1)
            g.memset(onesb[:], 1.0).then_inc(pads, 1)
            pool.wait_ge(pads, 5)
            g.affine_select(out=identb[:], in_=identb[:], compare_op=ALU.not_equal, fill=1.0, base=0,
                            pattern=[[-1, P]], channel_multiplier=1).then_inc(consts, 1)
            g.affine_select(out=maskb[:], in_=maskb[:], compare_op=ALU.is_ge, fill=MASKED, base=0,
                            pattern=[[-1, P]], channel_multiplier=1).then_inc(consts, 1)
            g.affine_select(out=beforeb[:], in_=beforeb[:], compare_op=ALU.is_ge, fill=1.0, base=0,
                            pattern=[[-1, P]], channel_multiplier=1).then_inc(consts, 1)
            pool.wait_ge(consts, 4)
            g.memset(kstack[ROWS:P], 1.0).then_inc(fills, 1)
            pool.wait_ge(fills, 1)
            g.memset(zeros, 0.0).then_inc(fills, 1)
            g.memset(vaug, 1.0).then_inc(fills, 1)
            g.memset(credit[:, 0:1], 0.0).then_inc(s_yfree, 1)
            g.memset(credit[:, 1:2], 0.0).then_inc(e_yr, 1)
            g.memset(credit[:, 2:3], 0.0).then_inc(e_out[0], DMA)
            g.memset(credit[:, 3:4], 0.0).then_inc(e_out[1], DMA)
            pool.wait_ge(ld_wvo, DMA * 4)
            pool.wait_ge(xs_ready, B)
            g.tensor_tensor(xs_all[:], xs_all[:],
                            bo_bc.rearrange("p (o d) -> p o d", o=1).to_broadcast([P, T, D]),
                            ALU.add).then_inc(bo_added, 1)

            def mask_batch(b):
                for s in range(NG):
                    for k in range(QT):
                        pool.wait_ge(b_free, B_ATT + b * B_PER + s * B_GRP + HP * (k + 1))
                        pool.sem_inc(mask_turn)
                        diag = pT[k][:, :, 0:P]
                        g.affine_select(out=diag, in_=diag, compare_op=ALU.is_ge, fill=0.0, base=0,
                                        pattern=[[0, HG], [1, P]], channel_multiplier=-1).then_inc(p_masked, 1)

            with pool.Fori(0, B) as b:
                mask_batch(b)

            pool.wait_ge(a_free, A_LOGITS)
            g.iota(io, [[0, T], [1, E]], base=0, channel_multiplier=0,
                   allow_small_or_imprecise_dtypes=True).then_inc(rconsts, 1)
            g.iota(io8, [[0, T], [1, E]], base=E, channel_multiplier=0,
                   allow_small_or_imprecise_dtypes=True).then_inc(rconsts, 1)
            g.iota(k128, [[0, E], [P, T]], base=0, channel_multiplier=0,
                   allow_small_or_imprecise_dtypes=True).then_inc(rconsts, 1)
            g.iota(tio, [[1, NT], [0, E]], base=0, channel_multiplier=0,
                   allow_small_or_imprecise_dtypes=True).then_inc(rconsts, 1)
            g.memset(upto, 1.0).then_inc(rconsts, 1)
            pool.wait_ge(rconsts, 5)
            g.affine_select(out=upto, in_=upto, compare_op=ALU.is_ge, fill=0.0, base=0,
                            pattern=[[1, E], [-1, E]], channel_multiplier=0).then_inc(rconsts, 1)

            pool.wait_ge(xg_zeroed, DMA)
            pool.wait_ge(slots_ready, TOP_K)
            for t in range(T):
                for k in range(TOP_K):
                    g.indirect_dma_start(xg, bass.IndirectOffsetOnAxis(slots[:, k, t:t + 1], 0),
                                         xn2[:, t, :], None).then_inc(scattered, DMA)
            for a in range(2):
                pool.wait_ge(e_out[a], DMA * ((NT - a + 1) // 2 + 1))
            for t in range(T):
                if t >= NYB:
                    pool.wait_ge(comb2, t - NYB + 1)
                for k in range(TOP_K):
                    g.indirect_dma_start(yb[:, t % NYB, k, :], None, yg,
                                         bass.IndirectOffsetOnAxis(slots[:, k, t:t + 1], 0)
                                         ).then_inc(y_in[t % NYB], DMA)

        @block.tensor
        def _(pe):
            mm, tr = nc.tensor.matmul, nc.tensor.transpose

            def ln_transposes(b, rows):
                for c in range(C):
                    for j in range(QT):
                        last = tr(Bk[:, 2 * (b % 2) + c, j * P:(j + 1) * P], rows(j, c), ident[:])
                last.then_inc(b_full, 1)

            def rowmax_scores(g, k, hp, n, par):
                pe.wait_ge(a_free, n - 1)
                w = (k + 1) * P
                dst = pair(A, par)
                for i in range(2):
                    h = g % 2 * HG + 2 * hp + i
                    mm(dst[:, i, 0:w], qstack[0:ROWS, g // 2, h, k * P:w], kstack[0:ROWS, g // 2, h, 0:w],
                       start=True, stop=False)
                    last = mm(dst[:, i, k * P:w], identb[:], maskb[:], start=False, stop=True)
                last.then_inc(a_full, 1)

            def maxima(n, par, g_count):
                pe.wait_ge(mparts_ready, g_count)
                pe.wait_ge(b_free, n - 1)
                for k in range(QT):
                    last = mm(pair(Bk, par)[0:3 * HG, 0, k * P:(k + 1) * P],
                              mparts[:, k].rearrange("p i h -> p (i h)"), identb[:], start=True, stop=True)
                last.then_inc(b_full, 1)

            def scoresT(g, k, hp, n, par):
                pe.wait_ge(b_free, n - 1)
                dst = pair(Bk, par)
                for i in range(2):
                    h = g % 2 * HG + 2 * hp + i
                    last = mm(dst[:, i, 0:S - k * P], kstack[0:ROWS + 3, g // 2, h, k * P:(k + 1) * P],
                              qstack[0:ROWS + 3, g // 2, h, k * P:S], start=True, stop=True)
                last.then_inc(b_full, 1)

            def probs_v(b, g, n, par):
                pe.wait_ge(b_free, n - 1)
                for k in range(QT):
                    pe.wait_ge(p_masked, (b * NG + g) * QT + k + 1)
                    for h in range(HG):
                        last = mm(pair(Bk, par)[32 * h:32 * h + 32, 0, k * P:S], vaug[:, k, HG * g + h, :],
                                  pT[k][:, h, :], start=k == 0, stop=k == QT - 1, tile_position=(0, 32 * h))
                last.then_inc(b_full, 1)

            def project_v(n, par, b):
                pe.wait_ge(a_free, n - 1)
                pe.wait_ge(ld_cv, DMA * (b + 1))
                for k in range(QT):
                    for c in range(C):
                        last = mm(pair(A, par)[:, k // 2, (k % 2) * D:(k % 2 + 1) * D],
                                  cV[:, c, k * P:(k + 1) * P], wv[:, c, :], start=c == 0, stop=c == C - 1)
                last.then_inc(a_full, 1)

            def project(par, a, half, b):
                w, src = ((wq, xnT), (wk, cT))[a]
                for c in range(C):
                    last = mm(pair(A, par)[:, a, :], w[:, c, half * P:(half + 1) * P],
                              src[:, c, bass.ds(b * S, S)], start=c == 0, stop=c == C - 1)
                return last

            pe.wait_ge(consts, 1)
            for b in range(B):
                pe.wait_ge(xs_ready, b + 1)
                if b >= 2:
                    pe.wait_ge(b_free, b - 1)
                ln_transposes(b, lambda j, c: xs[b % 2][:, j, c * P:(c + 1) * P])
                if b == 0:
                    pe.wait_ge(b_free, 1)
                    pe.wait_ge(ld_qk, 4 * DMA)
                    pe.wait_ge(ld_ctx0, DMA)
                    for half in range(2):
                        for a in range(2):
                            last = project(half, a, half, 0)
                        last.then_inc(a_full, 1)

            pe.wait_ge(ld_wvo, DMA * 4)
            project_v(2, 2, 0)
            pe.wait_ge(consts, 4)
            pe.wait_ge(fills, 3)
            pe.wait_ge(rows_in[0], DMA * 12)
            for j in range(A_GRP):
                rowmax_scores(0, QT - 1 - j // HP, j % HP, 3 + j, 3 + j)
            maxima(B_ATT - 1, B_ATT - 1, 1)
            pe.wait_ge(b_free, B)
            pe.wait_ge(ld_ctx, DMA * (B - 1))

            def batch(b, final):
                n_a, par_a = A_PRO + b * A_PER, A_PRO
                n_b, par_b = B_ATT + b * B_PER, B_ATT
                for s in range(NG):
                    ahead = not (final and s == NG - 1)
                    g1 = (s + 1) % NG
                    if s == 1 and not final:
                        pe.wait_ge(a_free, n_a - 1)
                        project(par_a, 0, 0, b + 1)
                        project(par_a, 1, 0, b + 1).then_inc(a_full, 1)
                        n_a, par_a = n_a + 1, par_a + 1
                    if ahead:
                        pe.wait_ge(rows_in[g1 // 2], DMA * 12 * (b + (2 if s == NG - 1 else 1)))
                        for j in range(LEAD):
                            rowmax_scores(g1, QT - 1 - j // HP, j % HP, n_a + j, par_a + j)
                    pe.wait_ge(max_in, DMA * (b * NG + s + 1))
                    for j in range(A_GRP):
                        scoresT(s, j // HP, j % HP, n_b + j, par_b + j)
                        j1 = j + LEAD
                        if ahead and j1 < A_GRP:
                            rowmax_scores(g1, QT - 1 - j1 // HP, j1 % HP, n_a + j1, par_a + j1)
                    n_b, par_b = n_b + A_GRP, par_b + A_GRP
                    if ahead:
                        n_a, par_a = n_a + A_GRP, par_a + A_GRP
                        maxima(n_b, par_b, b * NG + s + 2)
                        n_b, par_b = n_b + 1, par_b + 1
                    if s == 0:
                        pe.wait_ge(a_free, A_PRO + b * A_PER)
                    probs_v(b, s, n_b, par_b)
                    n_b, par_b = n_b + 1, par_b + 1
                if not final:
                    project_v(n_a, par_a, b + 1)
                    n_a, par_a = n_a + 1, par_a + 1
                pe.wait_ge(b_free, n_b)
                for i in range(2):
                    pe.wait_ge(a_free, n_a - 1)
                    for k in range(2):
                        for g in range(NG):
                            q = 2 * i + k
                            last = tr(pair(A, par_a)[:, k, g * P:(g + 1) * P], oT[:, g, q * P:(q + 1) * P], ident[:])
                    last.then_inc(a_full, 1)
                    n_a, par_a = n_a + 1, par_a + 1
                if not final:
                    pe.wait_ge(a_free, n_a - 1)
                    project(par_a, 0, 1, b + 1)
                pe.wait_ge(a_free, n_a)
                for c in range(C):
                    for k in range(QT):
                        last = tr(pair(Bk, par_b)[:, 0, k * P:(k + 1) * P], attn[:, k, c * P:(c + 1) * P], ident[:])
                    last.then_inc(b_full, 1)
                    n_b, par_b = n_b + 1, par_b + 1
                if not final:
                    project(par_a, 1, 1, b + 1).then_inc(a_full, 1)
                    n_a, par_a = n_a + 1, par_a + 1
                pe.wait_ge(b_free, n_b)
                for k in range(QT):
                    for c in range(C):
                        last = mm(pair(A, par_a)[:, k // 2, (k % 2) * D:(k % 2 + 1) * D],
                                  attnT[:, c, k * P:(k + 1) * P], wo[:, c, :], start=c == 0, stop=c == C - 1)
                last.then_inc(a_full, 1)

            with pe.Fori(0, B - 1) as b:
                batch(b, False)
            batch(B - 1, True)

            pe.wait_ge(a_free, A_LOGITS)
            pe.wait_ge(b_free, B_LN2)
            pe.wait_ge(ld_moe, DMA * (4 + M))

            def logits(b):
                pe.wait_ge(b_free, B_LN2 + b + 1)
                for t in range(b * QT, (b + 1) * QT):
                    for c in range(C):
                        last = mm(A[:, 0, t * E:(t + 1) * E], xn2T[:, c, t * P:(t + 1) * P], gw[:, c, :],
                                  start=c == 0, stop=c == C - 1)
                return last

            for b in range(B):
                pe.wait_ge(xs_ready, B + b + 1)
                if b >= 2:
                    pe.wait_ge(b_free, B_LN2 + b - 1)
                ln_transposes(b, lambda j, c: xn2[:, b * QT + j, c * P:(c + 1) * P])
                if b:
                    logits(b - 1)
            logits(B - 1).then_inc(a_full, 1)

            gu = [(A[:, 0, :], A[:, 1, :]), (A[:, 2, :], A[:, 3, :]), (Bk[:, 0, :], Bk[:, 1, :])]

            def shared_up(b):
                for m in range(M):
                    for w, dst in zip((wsg, wsu), gu[m]):
                        for c in range(C):
                            last = mm(dst, w[:, c, m * P:(m + 1) * P], xn2T[:, c, bass.ds(b * S, S)],
                                      start=c == 0, stop=c == C - 1)
                    last.then_inc(s_up, 1)

            def shared_down(b):
                pe.wait_ge(s_yfree, b + 1)
                for m in range(M):
                    pe.wait_ge(s_h, b * M + m + 1)
                    for j in range(QT):
                        last = mm(Bk[:, 2 + j // 2, (j % 2) * D:(j % 2 + 1) * D], hT[:, m, j * P:(j + 1) * P],
                                  wsd[:, m, :], start=m == 0 and j % 2 == 0, stop=m == M - 1,
                                  skip_group_check=True)
                last.then_inc(s_y, 1)

            pe.wait_ge(a_free, A_LOGITS + 1)
            shared_up(0)
            shared_down(0)
            shared_up(1)
            pe.wait_ge(sel_ready, 1)
            pe.wait_ge(s_yfree, 2)
            rank = Bk[:, 2, 0:TE].rearrange("p (t e) -> p t e", e=E)
            mm(rank, beforeb[:], selb, start=True, stop=False, skip_group_check=True)
            for s in range(1, T):
                mm(rank[:, s:T, :], onesb[:], selb[:, 0:T - s, :], start=False, stop=s == T - 1,
                   skip_group_check=True)
            for t in range(T):
                last = mm(Bk[:, 3, 0:E], onesb[:], selb[:, t, :], start=t == 0, stop=t == T - 1)
            last.then_inc(rank_full, 1)
            pe.wait_ge(slots_ready, TOP_K)
            shared_down(1)
            with pe.Fori(2, B) as b:
                shared_up(b)
                shared_down(b)

            def rows_t(a):
                for c in range(C):
                    last = tr(Bk[:, 0, c * P:(c + 1) * P], e_x[:, a, c * P:(c + 1) * P], ident[:])
                last.then_inc(e_xt, 1)

            def expert(t):
                return pe.value_load(expert_of[0:1, bass.ds(t, 1)], min_val=0, max_val=E - 1)

            def up(t, a, e):
                pe.wait_ge(e_xTr, t + 1)
                for i in range(2):
                    for c in range(C):
                        last = mm(A[:, 2 * a + i, 0:HALF], e_xT[:, a, c, :],
                                  wup[:, c, bass.ds(e * (2 * HALF) + i * HALF, HALF)],
                                  start=c == 0, stop=c == C - 1)
                last.then_inc(e_up, 1)

            def hidden_t(t, a):
                pe.wait_ge(e_hr, t + 1)
                for m in range(M):
                    last = tr(Bk[:, 1, m * P:(m + 1) * P], e_h[:, a, m * P:(m + 1) * P], ident[:])
                last.then_inc(e_ht, 1)

            def down(t, a, e):
                pe.wait_ge(e_hTr, t + 1)
                pe.wait_ge(e_yr, t + 1)
                for m in range(M):
                    last = mm(Bk[:, 2, 0:D], e_hT[:, a, m, :], wdn[:, m, bass.ds(e * D, D)],
                              start=m == 0, stop=m == M - 1)
                last.then_inc(e_yf, 1)

            pe.wait_ge(s_yfree, B + 1)
            pe.wait_ge(ld_up, DMA * C)
            pe.wait_ge(kept, 1)
            pe.wait_ge(e_in[0], DMA)
            rows_t(0)
            pe.wait_ge(e_in[1], DMA)
            pe.wait_ge(e_xTr, 1)
            rows_t(1)
            up(0, 0, expert(0))
            up(1, 1, expert(1))
            hidden_t(0, 0)
            pe.wait_ge(e_in[0], 2 * DMA)
            rows_t(0)
            up(2, 0, expert(2))
            with pe.Fori(0, (NT - 3) // 2) as i:
                t = 2 * i + 1
                e_down, e_up_ = expert(t - 1), expert(t + 2)
                pe.wait_ge(e_hTr, t)
                hidden_t(t, 1)
                pe.wait_ge(e_in[1], DMA * (i + 2))
                rows_t(1)
                down(t - 1, 0, e_down)
                up(t + 2, 1, e_up_)
                e_down, e_up_ = expert(t), expert(t + 3)
                pe.wait_ge(e_hTr, t + 1)
                hidden_t(t + 1, 0)
                pe.wait_ge(e_in[0], DMA * (i + 3))
                rows_t(0)
                down(t, 1, e_down)
                up(t + 3, 0, e_up_)
            e_last = [expert(t) for t in range(NT - 3, NT)]
            pe.wait_ge(e_hTr, NT - 2)
            hidden_t(NT - 2, 1)
            down(NT - 3, 0, e_last[0])
            pe.wait_ge(e_hTr, NT - 1)
            hidden_t(NT - 1, 0)
            down(NT - 2, 1, e_last[1])
            down(NT - 1, 0, e_last[2])

        @block.scalar
        def _(act):
            copy = lambda o, i: nc.scalar.activation(o, i, ACT.Copy)

            act.wait_ge(ln_step, 5)
            nc.scalar.activation(std[:], st_a[:], ACT.Sqrt).then_inc(std_ready, 1)

            def part1(u, n, w):
                if w is not None:
                    act.wait_ge(*w)
                for a in range(2):
                    act.wait_ge(*((val_ready, u + 1), (a_free, n + 1))[a])
                    copy(parts[:, a, 0, :], val[:, a, :]).then_inc(part1_ready, 1)

            def part2(u):
                for a in range(2):
                    act.wait_ge(rem_ready, 2 * u + a + 1)
                    copy(parts[:, a, 1, :], rem[:, a, :]).then_inc(part2_ready, 1)

            for b in range(B):
                act.wait_ge(b_full, b + 1)
                copy(xnT[:, :, b * S:(b + 1) * S], pair(Bk, b)).then_inc(b_free, 1)
                if b == 0:
                    part1(0, 0, None)
                    part2(0)
            part1(1, 1, (rows_in[0], DMA * 12))
            part2(1)

            def max_rows(n, par):
                act.wait_ge(b_full, n + 1)
                copy(mrows[0:3 * HG, :], pair(Bk, par)[0:3 * HG, 0, :]).then_inc(b_free, 1)

            def batch(b, final):
                n, par = B_ATT + b * B_PER, B_ATT
                for g in range(NG):
                    if g == 1 and not final:
                        part1(2 * b + 2, A_PRO + b * A_PER + A_GRP, (rows_in[1], DMA * 12 * (b + 1)))
                    for j in range(A_GRP):
                        k, hp = j // HP, j % HP
                        act.wait_ge(b_full, n + 1)
                        nc.scalar.activation(pT[k][:, 2 * hp:2 * hp + 2, :], pair(Bk, par)[:, :, 0:S - k * P],
                                             ACT.Exp).then_inc(b_free, 1)
                        n, par = n + 1, par + 1
                        if g == 1 and j == 1 and not final:
                            part2(2 * b + 2)
                    if not (final and g == NG - 1):
                        max_rows(n, par)
                        n, par = n + 1, par + 1
                    act.wait_ge(b_full, n + 1)
                    copy(oT[:, g, :], pair(Bk, par)[:, 0, :]).then_inc(b_free, 1)
                    n, par = n + 1, par + 1
                for c in range(C):
                    act.wait_ge(b_full, n + 1)
                    copy(attnT[:, c, :], pair(Bk, par)[:, 0, :]).then_inc(b_free, 1)
                    n, par = n + 1, par + 1
                if not final:
                    part1(2 * b + 3, A_PRO + (b + 1) * A_PER - 2, (rows_in[0], DMA * 12 * (b + 2)))
                    part2(2 * b + 3)

            max_rows(B_ATT - 1, B_ATT - 1)
            with act.Fori(0, B - 1) as b:
                batch(b, False)
            batch(B - 1, True)

            act.wait_ge(ln_step, 10)
            nc.scalar.activation(std[:], st_a[:], ACT.Sqrt).then_inc(std_ready, 1)
            for b in range(B):
                act.wait_ge(b_full, B_LN2 + b + 1)
                copy(xn2T[:, :, b * S:(b + 1) * S], pair(Bk, b)).then_inc(b_free, 1)

            act.wait_ge(d_ready, 1)
            nc.scalar.activation(ex, dl, ACT.Exp).then_inc(ex_ready, 1)
            gate = [A[:, 0, :], A[:, 2, :], Bk[:, 0, :]]
            with act.Fori(0, B) as b:
                for m in range(M):
                    act.wait_ge(s_up, b * M + m + 1)
                    nc.scalar.activation(sg[:, m, :], gate[m], ACT.Silu).then_inc(s_sg, 1)

            def rows_t(t, a):
                act.wait_ge(e_xt, t + 1)
                copy(e_xT[:, a], Bk[:, 0, 0:C * P].rearrange("p (c n) -> p c n", c=C)).then_inc(e_xTr, 1)

            def silu(t, a):
                act.wait_ge(e_up, t + 1)
                nc.scalar.activation(e_sg[:, a, :], A[:, 2 * a, 0:HALF], ACT.Silu).then_inc(e_sgr, 1)

            def hidden_t(t, a):
                act.wait_ge(e_ht, t + 1)
                copy(e_hT[:, a], Bk[:, 1, 0:M * P].rearrange("p (c n) -> p c n", c=M)).then_inc(e_hTr, 1)

            rows_t(0, 0)
            rows_t(1, 1)
            silu(0, 0)
            silu(1, 1)
            hidden_t(0, 0)
            rows_t(2, 0)
            silu(2, 0)
            with act.Fori(0, (NT - 3) // 2) as i:
                t = 2 * i + 1
                hidden_t(t, 1)
                rows_t(t + 2, 1)
                silu(t + 2, 1)
                hidden_t(t + 1, 0)
                rows_t(t + 3, 0)
                silu(t + 3, 0)
            hidden_t(NT - 2, 1)
            hidden_t(NT - 1, 0)

        @block.vector
        def _(dve):
            v = nc.vector

            def moments(first):
                me, mo, qe, qo = (stats[:, :, k] for k in (1, 4, 2, 5))
                dve.wait_ge(st_done, T * (1 if first else 2))
                base = 0 if first else 5
                v.tensor_tensor(mean[:], me, mo, ALU.add).then_inc(ln_step, 1)
                v.tensor_tensor(st_c[:], qe, qo, ALU.add).then_inc(ln_step, 1)
                v.tensor_tensor(st_a[:], me, mo, ALU.subtract).then_inc(ln_step, 1)
                dve.wait_ge(ln_step, base + 3)
                v.scalar_tensor_tensor(out=st_a[:], in0=st_a[:], scalar=0.25, in1=st_a[:], op0=ALU.mult,
                                       op1=ALU.mult).then_inc(ln_step, 1)
                v.tensor_scalar(mean[:], mean[:], 0.5, None, ALU.mult).then_inc(mean_done, 1)
                v.tensor_scalar(st_c[:], st_c[:], 1.0 / D, EPS, ALU.mult, ALU.add).then_inc(mean_done, 1)
                dve.wait_ge(ln_step, base + 4)
                dve.wait_ge(mean_done, 2 if first else 5)
                v.tensor_tensor(st_a[:], st_a[:], st_c[:], ALU.add).then_inc(ln_step, 1)
                dve.wait_ge(std_ready, 1 if first else 2)
                v.reciprocal(rstd[:], std[:]).then_inc(mean_done, 1)
                dve.wait_ge(mean_done, 3 if first else 6)

            def normalised(b, dst):
                for j in range(QT):
                    t = b * QT + j
                    last = v.tensor_scalar(dst(j), xs_all[:, bass.ds(t, 1), :], mean[:, bass.ds(t, 1)],
                                           rstd[:, bass.ds(t, 1)], ALU.subtract, ALU.mult)
                return last

            for b in range(B):
                dve.wait_ge(ld_x[b], DMA)
                for j in range(QT):
                    v.bn_stats(stats[:, b * QT + j, :], xs_all[:, b * QT + j, :]).then_inc(st_done, 1)
            moments(True)
            def values(n, half, par):
                dve.wait_ge(a_full, n + 1)
                for a, (bias, scale) in enumerate(((bqc, SCALE), (bkc, 1.0))):
                    last = v.tensor_scalar(val[:, a, :], pair(A, par)[:, a, :], bias[:, half:half + 1], scale,
                                           ALU.add, ALU.mult)
                    last.then_inc(a_free if a else val_ready, 1)

            def remainders(u):
                for a in range(2):
                    dve.wait_ge(part1_ready, 2 * u + a + 1)
                    v.tensor_tensor(rem[:, a, :], val[:, a, :], parts[:, a, 0, :], ALU.subtract).then_inc(rem_ready, 1)

            def part3(u):
                for a in range(2):
                    dve.wait_ge(part2_ready, 2 * u + a + 1)
                    last = v.tensor_tensor(parts[:, a, 2, :], rem[:, a, :], parts[:, a, 1, :], ALU.subtract)
                    last.then_inc(parts_ready, 1)

            for b in range(B):
                if b >= 2:
                    dve.wait_ge(b_full, b - 1)
                normalised(b, lambda j: xs[b % 2][:, j:j + 1, :]).then_inc(xs_ready, 1)
                if b == 1:
                    values(0, 0, 0)
                    remainders(0)
                    part3(0)
            values(1, 1, 1)
            remainders(1)
            part3(1)

            def add_v(n, par):
                dve.wait_ge(a_full, n + 1)
                vv = pair(A, par).rearrange("p a (k h i) -> p (a k) h i", k=2, h=H)
                bb = bv_bc.rearrange("p (o h i) -> p o h i", o=1, h=H).to_broadcast([P, QT, H, DK])
                v.tensor_tensor(vaug[:, :, :, 0:DK], vv, bb, ALU.add).then_inc(a_free, 1)

            dve.wait_ge(fills, 3)
            dve.wait_ge(ld_wvo, DMA * 4)
            add_v(2, 2)

            def rowmax(g, k, hp, n, par):
                dve.wait_ge(a_full, n + 1)
                v.tensor_reduce(mneg[:, k, 2 * hp:2 * hp + 2], pair(A, par)[:, :, 0:(k + 1) * P], AX.X, ALU.max,
                                negate=True).then_inc(a_free, 1)

            def max_parts(n, g_count):
                dve.wait_ge(a_free, n)
                s0 = (g_count - 1) * 3
                v.tensor_copy(mparts[:, :, 0, :], mneg).then_inc(mpart_step, 1)
                dve.wait_ge(mpart_step, s0 + 1)
                v.tensor_tensor(mrem, mneg, mparts[:, :, 0, :], ALU.subtract).then_inc(mpart_step, 1)
                dve.wait_ge(mpart_step, s0 + 2)
                v.tensor_copy(mparts[:, :, 1, :], mrem).then_inc(mpart_step, 1)
                dve.wait_ge(mpart_step, s0 + 3)
                v.tensor_tensor(mparts[:, :, 2, :], mrem, mparts[:, :, 1, :], ALU.subtract).then_inc(mparts_ready, 1)

            for j in range(A_GRP):
                rowmax(0, QT - 1 - j // HP, j % HP, 3 + j, 3 + j)
            max_parts(3 + A_GRP, 1)

            def batch(b, final):
                n, par = A_PRO + b * A_PER, A_PRO
                for s in range(NG):
                    splits = s == 1 and not final
                    if splits:
                        values(n, 0, par)
                        n, par = n + 1, par + 1
                    if final and s == NG - 1:
                        break
                    for j in range(A_GRP):
                        rowmax((s + 1) % NG, QT - 1 - j // HP, j % HP, n + j, par + j)
                        if splits and j == 1:
                            remainders(2 * b + 2)
                        if splits and j == 5:
                            part3(2 * b + 2)
                    n, par = n + A_GRP, par + A_GRP
                    max_parts(n, b * NG + s + 2)
                if not final:
                    add_v(n, par)
                    n, par = n + 1, par + 1
                for i in range(2):
                    dve.wait_ge(a_full, n + 1)
                    o = pair(A, par).rearrange("p k (h w) -> p k h w", w=32)
                    rci = rc[:, 2 * i:2 * i + 2, :]
                    v.reciprocal(rci, o[:, :, :, DK]).then_inc(rc_ready, 1)
                    dve.wait_ge(rc_ready, 2 * b + i + 1)
                    v.tensor_tensor(attn[:, 2 * i:2 * i + 2, :].rearrange("p k (h i) -> p k h i", h=H),
                                    o[:, :, :, 0:DK],
                                    rci.rearrange("p k (h o) -> p k h o", o=1).to_broadcast([P, 2, H, DK]),
                                    ALU.mult).then_inc(a_free, 1)
                    n, par = n + 1, par + 1
                if not final:
                    values(n, 1, par)
                    n, par = n + 1, par + 1
                    remainders(2 * b + 3)
                dve.wait_ge(a_full, n + 1)
                rows = xs_all[:, bass.ds(b * QT, QT), :]
                v.tensor_tensor(rows, pair(A, par).rearrange("p a (k d) -> p (a k) d", k=2), rows,
                                ALU.add).then_inc(a_free, 1)
                if not final:
                    part3(2 * b + 3)
                dve.wait_ge(a_free, n + 1)
                for j in range(QT):
                    v.bn_stats(stats[:, bass.ds(b * QT + j, 1), :],
                               xs_all[:, bass.ds(b * QT + j, 1), :]).then_inc(st_done, 1)

            dve.wait_ge(bo_added, 1)
            with dve.Fori(0, B - 1) as b:
                batch(b, False)
            batch(B - 1, True)

            moments(False)
            for b in range(B):
                normalised(b, lambda j: xn2[:, b * QT + j:b * QT + j + 1, :]).then_inc(xs_ready, 1)

            steps = [0]

            def link(ins):
                steps[0] += 1
                ins.then_inc(route, 1)
                dve.wait_ge(route, steps[0])

            def over_e(col):
                return col.rearrange("p (t o) -> p t o", o=1).to_broadcast([P, T, E])

            dve.wait_ge(a_full, A_LOGITS + 1)
            dve.wait_ge(rconsts, 6)
            v.tensor_copy(lg, A[:, 0, 0:TE].rearrange("p (t e) -> p t e", e=E)).then_inc(a_free, 1)

            def shared_h(b):
                for m in range(M):
                    dve.wait_ge(s_sg, b * M + m + 1)
                    up_ = (A[:, 1, :], A[:, 3, :], Bk[:, 1, :])[m]
                    v.tensor_tensor(hT[:, m, :], up_, sg[:, m, :], ALU.mult).then_inc(s_h, 1)

            def shared_y(b):
                dve.wait_ge(s_y, b + 1)
                rows = xs_all[:, bass.ds(b * QT, QT), :]
                v.tensor_tensor(rows, Bk[:, 2:4, :].rearrange("p a (k d) -> p (a k) d", k=2), rows,
                                ALU.add).then_inc(s_yfree, 1)

            dve.wait_ge(a_free, A_LOGITS + 1)
            link(v.tensor_reduce(m1, lg, AX.X, ALU.max))
            link(v.tensor_tensor(ra, lg, over_e(m1), ALU.is_equal))
            link(v.scalar_tensor_tensor(out=ra, in0=ra, scalar=-float(E), in1=io8, op0=ALU.mult, op1=ALU.add))
            link(v.tensor_reduce(i1, ra, AX.X, ALU.min))
            link(v.tensor_tensor(oh1, io, over_e(i1), ALU.is_equal))
            link(v.scalar_tensor_tensor(out=rb, in0=oh1, scalar=LOWEST, in1=lg, op0=ALU.mult, op1=ALU.add))
            link(v.tensor_reduce(m2, rb, AX.X, ALU.max))
            link(v.tensor_tensor(ra, rb, over_e(m2), ALU.is_equal))
            link(v.scalar_tensor_tensor(out=ra, in0=ra, scalar=-float(E), in1=io8, op0=ALU.mult, op1=ALU.add))
            link(v.tensor_reduce(i2, ra, AX.X, ALU.min))
            link(v.tensor_tensor(oh2, io, over_e(i2), ALU.is_equal))
            v.tensor_tensor(dl, m2, m1, ALU.subtract).then_inc(d_ready, 1)
            v.tensor_tensor(selb, oh1, oh2, ALU.add).then_inc(sel_ready, 1)
            dve.wait_ge(ex_ready, 1)
            link(v.tensor_scalar(sm, ex, 1.0, None, ALU.add))
            link(v.reciprocal(wts[:, 0, :], sm))
            link(v.tensor_tensor(wts[:, 1, :], ex, wts[:, 0, :], ALU.mult))
            shared_h(0)
            shared_y(0)

            dve.wait_ge(rank_full, 1)
            link(v.tensor_copy(tot, Bk[:, 3, 0:E]))
            link(v.tensor_tensor(k128, tot.rearrange("p (e o) -> p e o", o=1).to_broadcast([P, E, T]), k128,
                                 ALU.is_gt))
            link(v.tensor_reduce(tiles_of, k128, AX.X, ALU.add))
            link(v.tensor_tensor(ee, tiles_of.rearrange("p (o e) -> p o e", o=1).to_broadcast([P, E, E]), upto,
                                 ALU.mult))
            link(v.tensor_reduce(ends, ee, AX.X, ALU.add))
            link(v.tensor_tensor(base, ends, tiles_of, ALU.subtract))
            link(v.scalar_tensor_tensor(
                out=rslot, in0=base.rearrange("p (o e) -> p o e", o=1).to_broadcast([P, T, E]), scalar=float(P),
                in1=Bk[:, 2, 0:TE].rearrange("p (t e) -> p t e", e=E), op0=ALU.mult, op1=ALU.add))
            link(v.tensor_tensor(tcmp, ends.rearrange("p (o e) -> p o e", o=1).to_broadcast([P, NT, E]), tio,
                                 ALU.is_le))
            link(v.tensor_reduce(tnum, tcmp, AX.X, ALU.add))
            v.tensor_scalar(expert_of[:], tnum, float(E - 1), None, ALU.min).then_inc(kept, 1)
            for k, oh in enumerate((oh1, oh2)):
                link(v.tensor_tensor(oh, oh, rslot, ALU.mult))
                link(v.tensor_reduce(slotf[:, k, :], oh, AX.X, ALU.add))
                v.tensor_copy(slots[:, k, :], slotf[:, k, :]).then_inc(slots_ready, 1)

            with dve.Fori(1, B) as b:
                shared_h(b)
                shared_y(b)

            def hidden(t, a):
                dve.wait_ge(e_sgr, t + 1)
                v.tensor_tensor(e_h[:, a, :], A[:, 2 * a + 1, 0:HALF], e_sg[:, a, :], ALU.mult).then_inc(e_hr, 1)

            def result(t, a, i):
                dve.wait_ge(e_yf, t + 1)
                dve.wait_ge(e_out[a], DMA * (i + 1))
                v.tensor_copy(e_y[:, a, :], Bk[:, 2, 0:D]).then_inc(e_yr, 1)

            hidden(0, 0)
            hidden(1, 1)
            hidden(2, 0)
            with dve.Fori(0, (NT - 3) // 2) as i:
                t = 2 * i + 1
                result(t - 1, 0, i)
                hidden(t + 2, 1)
                result(t, 1, i)
                hidden(t + 3, 0)
            result(NT - 3, 0, (NT - 3) // 2)
            result(NT - 2, 1, (NT - 3) // 2)
            result(NT - 1, 0, (NT - 1) // 2)

            for t in range(T):
                dve.wait_ge(y_in[t % NYB], DMA * TOP_K * (t // NYB + 1))
                row = xs_all[:, t, :]
                v.scalar_tensor_tensor(out=row, in0=yb[:, t % NYB, 0, :], scalar=wts[:, 0, t:t + 1], in1=row,
                                       op0=ALU.mult, op1=ALU.add).then_inc(comb1, 1)
                dve.wait_ge(comb1, t + 1)
                v.scalar_tensor_tensor(out=row, in0=yb[:, t % NYB, 1, :], scalar=wts[:, 1, t:t + 1], in1=row,
                                       op0=ALU.mult, op1=ALU.add).then_inc(comb2, 1)


def kernel(x, ctx_1024, L0_xattn_Wq, L0_xattn_bq, L0_xattn_Wk, L0_xattn_bk, L0_xattn_Wv, L0_xattn_bv,
           L0_xattn_Wo, L0_xattn_bo, L0_ffn_gate_w, L0_ffn_w_up, L0_ffn_w_down, L0_ffn_sg_gate,
           L0_ffn_sg_up, L0_ffn_sg_down):
    import numpy as np
    import concourse.bacc as bacc
    from concourse.bass_utils import run_bass_kernel_spmd

    def by_half(a):
        return np.transpose(np.reshape(a, (-1, 2, NUM_HEADS // 2, a.shape[-1] // NUM_HEADS)),
                            (0, 1, 3, 2)).reshape(-1, a.shape[-1])

    arrays = {
        "x": x,
        "ctxT": np.transpose(ctx_1024, (0, 2, 1)),
        "wqT": by_half(np.transpose(L0_xattn_Wq)), "bq": np.transpose(by_half(L0_xattn_bq).reshape(2, -1)),
        "wkT": by_half(np.transpose(L0_xattn_Wk)), "bk": np.transpose(by_half(L0_xattn_bk).reshape(2, -1)),
        "wvT": np.transpose(L0_xattn_Wv), "bv": L0_xattn_bv,
        "woT": np.transpose(L0_xattn_Wo), "bo": L0_xattn_bo,
        "gwT": np.transpose(L0_ffn_gate_w),
        "wupT": np.transpose(L0_ffn_w_up, (2, 0, 1)).reshape(L0_ffn_w_up.shape[2], -1),
        "wdnT": np.transpose(L0_ffn_w_down, (2, 0, 1)).reshape(L0_ffn_w_down.shape[2], -1),
        "sgT": np.transpose(L0_ffn_sg_gate),
        "suT": np.transpose(L0_ffn_sg_up),
        "sdT": np.transpose(L0_ffn_sg_down),
    }
    arrays = {k: np.ascontiguousarray(v) for k, v in arrays.items()}
    nc = bacc.Bacc("TRN2", target_bir_lowering=False, num_devices=1)
    aps = {k: nc.dram_tensor(f"in_{k}", a.shape, mybir.dt.from_np(a.dtype), kind="ExternalInput").ap()
           for k, a in arrays.items()}
    out = nc.dram_tensor("out", x.shape, mybir.dt.from_np(np.dtype(x.dtype)), kind="ExternalOutput").ap()
    build(nc, *aps.values(), out)
    r = run_bass_kernel_spmd(nc, [{f"in_{k}": a for k, a in arrays.items()}], core_ids=[0])
    return r.results[0]["out"]
```

```python
from contextlib import ExitStack

import concourse.bass as bass
from concourse import mybir

P = 128
F32 = mybir.dt.float32
F32R = mybir.dt.float32r
BF16 = mybir.dt.bfloat16
I32 = mybir.dt.int32
ALU = mybir.AluOpType
ACT = mybir.ActivationFunctionType
AX = mybir.AxisListType

NUM_HEADS = 16
EPS = 1e-5
MASKED = -1e30
LOWEST = -3e38
DMA = 16


def build(nc, x, ctxT, wqT, bq, wkT, bk, wvT, bv, woT, bo, gwT, wupT, wdnT, sgT, suT, sdT, out):
    B, S, D = x.shape
    H = NUM_HEADS
    DK = D // H
    HG = P // 32
    NG = H // HG
    HH = P // DK
    C = D // P
    QT = S // P
    N = B * S
    T = N // P
    E = gwT.shape[1]
    HALF = sgT.shape[1]
    M = HALF // P
    TOP_K = 2
    NT = (TOP_K * N + E * (P - 1)) // P
    NT += 1 - NT % 2
    N_SHARED_1 = B - 1
    Z = NT // (4 * (B - 1) + 1)
    assert NT == Z * (4 * (B - 1) + 1) and M == B - 1
    SCALE = float(DK) ** -0.5
    Q_PART = (0, 0, 1, 1, 0, 2)
    K_PART = (0, 1, 0, 1, 2, 0)
    ROWS = DK * len(Q_PART)
    assert S == 512 and D == 256 and H == 2 * HH and ROWS == 96

    with ExitStack() as ctx:
        def sb(name, shape, dt=F32):
            return ctx.enter_context(nc.sbuf_tensor(name, shape, dt))

        def sem(name):
            return ctx.enter_context(nc.semaphore(name))

        XW = D + 2
        xg = nc.dram_tensor("x_by_slot", (NT * P, XW), F32, kind="Internal").ap()
        yc = nc.dram_tensor("y_by_choice", (3 * N + P, D), F32, kind="Internal").ap()

        A = ctx.enter_context(nc.psum_tensor("set_a", [P, 4, 512], F32))
        Bk = ctx.enter_context(nc.psum_tensor("set_b", [P, 4, 512], F32))
        pv_bank = Bk[:, 3, :]

        xs_all = sb("x_res", [P, T, D])
        wdn = sb("w_down", [P, M, E * D])
        wsg = sb("w_sg", [P, C, HALF])
        wsu = sb("w_su", [P, C, HALF])
        wsd = sb("w_sd", [P, M, D])
        gw = sb("gate_w", [P, C, E])
        ident = sb("ident", [P, P])
        identb = sb("identb", [P, P], BF16)
        maskb = sb("maskb", [P, P], BF16)
        beforeb = sb("beforeb", [P, P], BF16)
        onesb = sb("onesb", [P, P], BF16)
        slots = sb("slots", [P, TOP_K, T], I32)
        wts = sb("wts", [P, TOP_K, T])
        expert_of = sb("expert_of", [P, NT], I32)
        expert_f = sb("expert_f", [P, NT])
        e_who = sb("e_who", [P, 2, 2])
        e_second = sb("e_second", [P, 2])
        e_dst = sb("e_dst", [P, 2], I32)
        stats = sb("stats", [P, T, 6])
        st_a = sb("st_a", [P, T])
        st_c = sb("st_c", [P, T])
        mean = sb("mean", [P, T])
        rstd = sb("rstd", [P, T])
        std = sb("std", [P, T])

        credit = sb("credit", [P, 2])

        KB = 256
        REGION = 140 * KB
        with nc.sbuf_tensor("attention", [P, REGION], F32) as attention:
            pass
        MOE = 39 * KB
        moe = sb("moe", [P, MOE])
        e_xT_hi = sb("e_xT_hi", [P, 2, C, P], F32R)
        e_xT_lo = sb("e_xT_lo", [P, 2, C, P], F32R)
        ROUTER = 10 * KB
        with nc.sbuf_tensor("router", [P, ROUTER], F32) as router:
            pass
        wup_hi = sb("wup_hi", [P, C, E * 2 * HALF], F32R)
        with nc.sbuf_tensor("wup", [P, C, E * 2 * HALF], F32) as wup:
            pass
        wup_lo = sb("wup_lo", [P, C, E * 2 * HALF], F32R)
        region, size, used = [attention], [REGION], [0]

        def part(words):
            lo = used[0]
            used[0] += words
            assert used[0] <= size[0], used[0] / KB
            return region[0][:, lo:lo + words]

        def parts_of(tensor, words):
            region[0], size[0], used[0] = tensor, words, 0

        xnT = part(C * N).rearrange("p (c n) -> p c n", c=C)
        cT = part(C * N).rearrange("p (c n) -> p c n", c=C)
        pT_at = [sum(HG * (S - P * j) for j in range(k)) for k in range(QT + 1)]
        pT_all = part(pT_at[QT])
        pT = [pT_all[:, pT_at[k]:pT_at[k + 1]].rearrange("p (h q) -> p h q", h=HG) for k in range(QT)]
        qstack = part(2 * HH * S // 2).bitcast(BF16).rearrange("p (a h n) -> p a h n", a=2, h=HH)
        kstack = part(2 * HH * S // 2).bitcast(BF16).rearrange("p (a h n) -> p a h n", a=2, h=HH)
        val = part(2 * S).rearrange("p (a n) -> p a n", a=2)
        rem = part(2 * S).rearrange("p (a n) -> p a n", a=2)
        parts = part(2 * 3 * S // 2).bitcast(BF16).rearrange("p (a i n) -> p a i n", a=2, i=3)
        mneg = part(QT * HG).rearrange("p (k h) -> p k h", k=QT)
        mrem = part(QT * HG).rearrange("p (k h) -> p k h", k=QT)
        mparts = part(QT * 3 * HG // 2).bitcast(BF16).rearrange("p (k i h) -> p k i h", k=QT, i=3)
        mrows = part(S // 2).bitcast(BF16)
        vaug = part(QT * H * 32).rearrange("p (k h w) -> p k h w", k=QT, h=H)
        oT = part(NG * S).rearrange("p (g n) -> p g n", g=NG)
        attn = part(QT * D).rearrange("p (k d) -> p k d", k=QT)
        attnT = part(C * S).rearrange("p (c n) -> p c n", c=C)
        cV = part(C * S).rearrange("p (c n) -> p c n", c=C)
        wq = part(C * D).rearrange("p (c n) -> p c n", c=C)
        wk = part(C * D).rearrange("p (c n) -> p c n", c=C)
        wv = part(C * D).rearrange("p (c n) -> p c n", c=C)
        wo = part(C * D).rearrange("p (c n) -> p c n", c=C)
        bv_bc = part(D)
        bo_bc = part(D)
        rc = part(QT * H).rearrange("p (k h) -> p k h", k=QT)
        bqc = part(2)
        bkc = part(2)
        zeros = part(XW)
        xs = [attn, attnT.rearrange("p c (k d) -> p (c k) d", d=D)]

        parts_of(moe, MOE)
        xn2 = part(T * XW).rearrange("p (t d) -> p t d", t=T)
        xn2T = part(C * N).rearrange("p (c n) -> p c n", c=C)
        sg = part(M * S).rearrange("p (m n) -> p m n", m=M)
        lgT = [sg[0:E, b % M, :] for b in range(B)]
        TE = T * E
        parts_of(moe, C * N)
        e_x = part(2 * D).rearrange("p (a d) -> p a d", a=2)
        e_sg = part(2 * HALF).rearrange("p (a d) -> p a d", a=2)
        e_h = part(2 * HALF).rearrange("p (a d) -> p a d", a=2)
        e_hT = part(2 * M * P).rearrange("p (a c n) -> p a c n", a=2, c=M)
        e_y = part(2 * D).rearrange("p (a d) -> p a d", a=2)
        NYB = 4
        yb = [xn2T[:, 0, a * S:(a + 1) * S].rearrange("p (k d) -> p k d", k=TOP_K) for a in range(3)]
        yb += [xn2T[:, 1, 0:S].rearrange("p (k d) -> p k d", k=TOP_K)]
        parts_of(router, ROUTER)

        def te():
            return part(TE).rearrange("p (t e) -> p t e", e=E)

        lg, io, io8, oh1, oh2, ra, rb, rslot = (te() for _ in range(8))
        selb = part(TE // 2).bitcast(BF16).rearrange("p (t e) -> p t e", e=E)
        m1, m2, i1, i2, dl, ex, sm = (part(T) for _ in range(7))
        k128 = part(E * T).rearrange("p (e k) -> p e k", e=E)
        upto = part(E * E).rearrange("p (a b) -> p a b", a=E)
        tot, tiles_of, ends, base = (part(E) for _ in range(4))
        ee = part(E * E).rearrange("p (a b) -> p a b", a=E)
        tio = part(NT * E).rearrange("p (t e) -> p t e", e=E)
        tcmp = part(NT * E).rearrange("p (t e) -> p t e", e=E)
        tnum = part(NT)
        slotf = part(TOP_K * T).rearrange("p (k t) -> p k t", k=TOP_K)

        ld_x = [sem(f"ld_x{b}") for b in range(B)]
        ld_k, ld_q, ld_ctx, ld_v, ld_o, ld_cv, ld_moe, ld_up = (sem(n) for n in
            ("ld_k", "ld_q", "ld_ctx", "ld_v", "ld_o", "ld_cv", "ld_moe", "ld_up"))
        xg_zeroed = sem("xg_zeroed")
        consts, pads, fills, pad_rows = sem("consts"), sem("pads"), sem("fills"), sem("pad_rows")
        st_done, ln_step, std_ready, xs_ready = sem("st_done"), sem("ln_step"), sem("std_ready"), sem("xs_ready")
        mean_done = sem("mean_done")
        val_ready, part1_ready, rem_ready, part2_ready, parts_ready = (sem(n) for n in
            ("val_ready", "part1_ready", "rem_ready", "part2_ready", "parts_ready"))
        rows_in = [sem("rows_in0"), sem("rows_in1")]
        mpart_step, mparts_ready, max_in = (sem(n) for n in
            ("mpart_step", "mparts_ready", "max_in"))
        bo_added = sem("bo_added")
        pv_full, pv_free = sem("pv_full"), sem("pv_free")
        a_full, a_free, b_full, b_free = sem("a_full"), sem("a_free"), sem("b_full"), sem("b_free")
        p_masked, rc_ready, pool_turns = sem("p_masked"), sem("rc_ready"), sem("pool_turns")
        lt_full, lt_read, lg_read, logits_full, route, d_ready, ex_ready, sel_ready = (sem(n) for n in
            ("lt_full", "lt_read", "lg_read", "logits_full", "route", "d_ready", "ex_ready", "sel_ready"))
        rank_full, slots_ready = sem("rank_full"), sem("slots_ready")
        rconsts, scattered, experts_known = sem("rconsts"), sem("scattered"), sem("experts_known")
        s_up, s_sg, s_h, s_y, s_yfree = (sem(n) for n in ("s_up", "s_sg", "s_h", "s_y", "s_yfree"))
        e_in = [sem("e_in0"), sem("e_in1")]
        who_in = [sem("who_in0"), sem("who_in1")]
        second, dst_ready = sem("second"), sem("dst_ready")
        e_out = [sem("e_out0"), sem("e_out1")]
        up_hi, up_lo, wts_ready, e_xhi = (sem(n) for n in ("up_hi", "up_lo", "wts_ready", "e_xhi"))
        e_xt, e_xTr, e_up, e_sgr, e_hr, e_ht, e_hTr, e_yf, e_yr = (sem(n) for n in
            ("e_xt", "e_xTr", "e_up", "e_sgr", "e_hr", "e_ht", "e_hTr", "e_yf", "e_yr"))
        y_in = [sem(f"y_in{i}") for i in range(NYB)]
        comb1, comb2, stored = sem("comb1"), sem("comb2"), sem("stored")

        def heads_in_pair(k):
            return max(2, min(HG, 1024 // ((k + 1) * P)) & ~1)

        def heads_in_bank(k):
            return 1 if k < 2 else min(HG, 512 // (S - k * P))

        R_JOBS = [(k, h, heads_in_pair(k)) for k in range(QT - 1, -1, -1) for h in range(0, HG, heads_in_pair(k))]
        A_GRP = len(R_JOBS)
        A_PRO = 3 + 2 * A_GRP
        A_PER = NG * A_GRP + 2 + 2 + 1 + 1
        A_ALL = A_PRO + B * A_PER - 2 * A_GRP - 3
        S_JOBS = [(k, h, heads_in_bank(k)) for k in range(QT) for h in range(0, HG, heads_in_bank(k))]
        S_N = len(S_JOBS)
        B_SLOT = S_N + 1
        SLOT = [("R", 0), ("PV", 0), ("R", 1), ("PV", 1), ("R", 2),
                ("S", 0), ("R", 3), ("S", 1), ("R", 4), ("S", 2), ("S", 3), ("R", 5), ("S", 4), ("S", 5),
                ("S", 6), ("S", 7), ("PV", 2), ("PV", 3), ("S", 8), ("MAX", 0), ("S", 9), ("S", 10)]
        LOGITS_IN = [A[:, 0, :], A[:, 1, :], pv_bank, A[:, 0, :]]
        assert A_ALL % 2 == 0
        MAX_AT = 9
        assert [n for kind, n in SLOT if kind == "R"] == list(range(A_GRP))
        assert [n for kind, n in SLOT if kind == "S"] == list(range(S_N))
        A_TILES = [range(i, min(i + 3, C * QT)) for i in range(0, C * QT, 3)]
        NA = len(A_TILES)
        LN_JOB, LN_PAIR, MAX_0 = (0, 2, 3, 4), (0, 0, 1, 0), 1
        B_GRP0 = B + 1
        B_ATT = B_GRP0 + B_SLOT
        B_PER = NG * B_SLOT + NA
        B_LAST = B_ATT + B * B_PER - B_SLOT - 1 - NA
        B_LN2 = [B_LAST, B_LAST + C, B_LAST + 2 * C + NA, B_LAST + 3 * C + NA]
        assert B == 4
        assert A_PER % 2 == 0 and B_PER % 3 == 0 and B_SLOT % 3 == 0

        def bank(par):
            return Bk[:, (par - B) % 3, :]

        def pair(bank_set, n):
            return bank_set[:, n % 2 * 2:n % 2 * 2 + 2, :]

        SPLITS = 8
        SPLIT_AT = [range(0, 4), range(4, SPLITS)] + [()] * (N_SHARED_1 - 2)

        def piece(w, i):
            cut = C * E * 2 * HALF // SPLITS
            return w[:].rearrange("p c n -> p (c n)")[:, i * cut:(i + 1) * cut]

        block = ctx.enter_context(nc.Block())

        @block.sync
        def _(sp):
            x_t = x.rearrange("b (k p) d -> b p k d", p=P)
            def load_x(b):
                sp.dma_start(xs_all[:, b * QT:(b + 1) * QT, :], x_t[b]).then_inc(ld_x[b], DMA)

            def load_ctx(b, done):
                sp.dma_start(cT[:, :, b * S:(b + 1) * S],
                             ctxT[b].rearrange("(c p) n -> p c n", p=P)[:, :, 0:S]).then_inc(done, DMA)

            load_x(0)
            sp.dma_start(wk, wkT.rearrange("(c p) n -> p c n", p=P)).then_inc(ld_k, DMA)
            load_ctx(0, ld_k)
            sp.dma_start(wq, wqT.rearrange("(c p) n -> p c n", p=P)).then_inc(ld_q, DMA)
            sp.dma_start(bqc, bq).then_inc(ld_q, DMA)
            sp.dma_start(bkc, bk).then_inc(ld_q, DMA)
            load_x(1)
            sp.dma_start(wv, wvT.rearrange("(c p) n -> p c n", p=P)).then_inc(ld_v, DMA)
            sp.dma_start(bv_bc, bv.partition_broadcast(P)).then_inc(ld_v, DMA)
            for b in range(2, B):
                load_x(b)
            for b in range(1, B):
                load_ctx(b, ld_ctx)
            sp.dma_start(wo, woT.rearrange("(c p) n -> p c n", p=P)).then_inc(ld_o, DMA)
            sp.dma_start(bo_bc, bo.partition_broadcast(P)).then_inc(ld_o, DMA)

            def stack(half, u):
                for a, (dst, order) in enumerate(((qstack, Q_PART), (kstack, K_PART))):
                    sp.wait_ge(parts_ready, 2 * u + a + 1)
                    for j, part_of in enumerate(order):
                        sp.dma_start(dst[DK * j:DK * (j + 1), half, :, :],
                                     parts[:, a, part_of, :]).then_inc(rows_in[half], DMA)

            def max_rows(g, n):
                sp.wait_ge(b_free, n + 1)
                h = g % 2 * HG
                sp.dma_start(qstack[ROWS:ROWS + 3, g // 2, h:h + HG, :], mrows[0:3 * HG, :]).then_inc(max_in, DMA)

            stack(0, 0)
            stack(1, 1)
            def zero_rows(piece):
                sp.dma_start(xg[bass.ds(piece * Z * P, Z * P), :].rearrange("(t p) d -> p t d", p=P),
                             zeros.rearrange("p (o d) -> p o d", o=1).to_broadcast([P, Z, XW])
                             ).then_inc(xg_zeroed, DMA)

            max_rows(0, MAX_0)

            def batch(b, final):
                n_b = B_ATT + b * B_PER
                if not final:
                    sp.wait_ge(a_full, A_PRO + b * A_PER - 1)
                    sp.dma_start(cV, ctxT[bass.ds(b + 1, 1)].rearrange("o (c p) n -> p (o c) n", p=P)[:, :, 0:S]
                                 ).then_inc(ld_cv, DMA)
                max_rows(2, n_b + MAX_AT)
                if not final:
                    zero_rows(4 * b + 1)
                    sp.wait_ge(b_full, n_b + B_SLOT)
                    stack(0, 2 * b + 2)
                max_rows(3, n_b + B_SLOT + MAX_AT)
                if final:
                    for w, w_dram in ((wsg, sgT), (wsu, suT), (wsd, sdT), (gw, gwT)):
                        sp.dma_start(w[:], w_dram.rearrange("(c p) n -> p c n", p=P)).then_inc(ld_moe, DMA)
                else:
                    zero_rows(4 * b + 2)
                    zero_rows(4 * b + 3)
                    max_rows(0, n_b + 2 * B_SLOT + MAX_AT)
                    zero_rows(4 * b + 4)
                    sp.wait_ge(b_full, n_b + 3 * B_SLOT)
                    stack(1, 2 * b + 3)
                    max_rows(1, n_b + 3 * B_SLOT + MAX_AT)
                    sp.dma_start(wdn[:, bass.ds(b, 1), :], wdnT[bass.ds(b * P, P)].rearrange("p (o n) -> p o n", o=1)
                                 ).then_inc(ld_moe, DMA)

            sp.wait_ge(pad_rows, 1)
            zero_rows(0)
            max_rows(1, B_GRP0 + MAX_AT)
            with sp.Fori(0, B - 1) as b:
                batch(b, False)
            batch(B - 1, True)
            sp.wait_ge(a_free, A_ALL)
            for c in range(C):
                sp.dma_start(wup[:, c, :], wupT[c * P:(c + 1) * P]).then_inc(ld_up, DMA)

            xg_t = xg.rearrange("(t p) d -> t p d", p=P)
            sp.wait_ge(scattered, DMA * TOP_K * T)
            for a in range(2):
                sp.dma_start(e_x[:, a, :], xg_t[a][:, 0:D]).then_inc(e_in[a], DMA)
            for a in range(2):
                sp.dma_start(e_who[:, a, :], xg_t[a][:, D:XW]).then_inc(who_in[a], DMA)
            for t in range(2, 5):
                sp.wait_ge(e_xt, t - 1)
                sp.dma_start(e_x[:, t % 2, :], xg_t[t][:, 0:D]).then_inc(e_in[t % 2], DMA)
            with sp.Fori(0, (NT - 5) // 2) as i:
                for a in (1, 0):
                    t = 2 * i + (1 if a else 2)
                    sp.wait_ge(e_xt, t + 3)
                    sp.dma_start(e_x[:, a, :], xg[bass.ds((t + 4) * P, P), 0:D]).then_inc(e_in[a], DMA)
                    sp.wait_ge(dst_ready, t)
                    sp.dma_start(e_who[:, 1 - a, :], xg[bass.ds((t + 1) * P, P), D:XW]).then_inc(who_in[1 - a], DMA)
            for t in range(NT - 3, NT):
                sp.wait_ge(dst_ready, t - 1)
                sp.dma_start(e_who[:, t % 2, :], xg_t[t][:, D:XW]).then_inc(who_in[t % 2], DMA)

            def results_in(t):
                sp.dma_start(yb[t % NYB], yc[0:TOP_K * N].rearrange("(k t p) d -> t p k d", k=TOP_K, p=P)[t]
                             ).then_inc(y_in[t % NYB], DMA)

            for a in range(2):
                sp.wait_ge(e_out[a], DMA * ((NT - a + 1) // 2))
            o_t = out.rearrange("b (k p) d -> (b k) p d", p=P)
            for t in range(NYB):
                results_in(t)
            for t in range(T):
                sp.wait_ge(comb2, t + 1)
                sp.dma_start(o_t[t], xs_all[:, t, :]).then_inc(stored, DMA)
                if t + NYB < T:
                    results_in(t + NYB)
            sp.wait_ge(stored, DMA * T)

        @block.gpsimd
        def _(pool):
            g = nc.gpsimd
            g.memset(ident[:], 0.0).then_inc(pads, 1)
            pool.wait_ge(pads, 1)
            g.affine_select(out=ident[:], in_=ident[:], compare_op=ALU.not_equal, fill=1.0, base=0,
                            pattern=[[-1, P]], channel_multiplier=1).then_inc(consts, 1)
            g.memset(identb[:], 0.0).then_inc(pads, 1)
            g.memset(maskb[:], 0.0).then_inc(pads, 1)
            g.memset(beforeb[:], 0.0).then_inc(pads, 1)
            g.memset(onesb[:], 1.0).then_inc(pads, 1)
            pool.wait_ge(pads, 5)
            g.affine_select(out=identb[:], in_=identb[:], compare_op=ALU.not_equal, fill=1.0, base=0,
                            pattern=[[-1, P]], channel_multiplier=1).then_inc(consts, 1)
            g.affine_select(out=maskb[:], in_=maskb[:], compare_op=ALU.is_ge, fill=MASKED, base=0,
                            pattern=[[-1, P]], channel_multiplier=1).then_inc(consts, 1)
            g.affine_select(out=beforeb[:], in_=beforeb[:], compare_op=ALU.is_ge, fill=1.0, base=0,
                            pattern=[[-1, P]], channel_multiplier=1).then_inc(consts, 1)
            pool.wait_ge(consts, 4)
            g.memset(kstack[ROWS:P], 1.0).then_inc(fills, 1)
            pool.wait_ge(fills, 1)
            g.memset(zeros, 0.0).then_inc(fills, 1)
            g.memset(vaug, 1.0).then_inc(fills, 1)
            pool.wait_ge(fills, 2)
            g.iota(zeros[:, D:D + 1], [[0, 1]], base=2 * N, channel_multiplier=1,
                   allow_small_or_imprecise_dtypes=True).then_inc(pad_rows, 1)
            g.memset(credit[:, 0:1], 0.0).then_inc(s_yfree, 1)
            g.memset(credit[:, 1:2], 0.0).then_inc(e_yr, 1)
            pool.wait_ge(ld_o, DMA * 2)
            pool.wait_ge(xs_ready, B)
            g.tensor_tensor(xs_all[:], xs_all[:],
                            bo_bc.rearrange("p (o d) -> p o d", o=1).to_broadcast([P, T, D]),
                            ALU.add).then_inc(bo_added, 1)

            def pool_turn(signal, count):
                pool.wait_ge(signal, count)
                pool.sem_inc(pool_turns)

            def remainders(u):
                for a in range(2):
                    pool_turn(part1_ready, 2 * u + a + 1)
                    g.tensor_tensor(rem[:, a, :], val[:, a, :], parts[:, a, 0, :], ALU.subtract).then_inc(rem_ready, 1)

            def part3(u):
                for a in range(2):
                    pool_turn(part2_ready, 2 * u + a + 1)
                    g.tensor_tensor(parts[:, a, 2, :], rem[:, a, :], parts[:, a, 1, :],
                                    ALU.subtract).then_inc(parts_ready, 1)

            def mask_group(n, last=False, split=None):
                if split is not None:
                    remainders(split)
                for k in range(QT):
                    if k == 2 and split is not None:
                        part3(split)
                    jobs = sum(job[0] <= k for job in S_JOBS)
                    pool_turn(b_free, n + jobs + (1 if jobs > MAX_AT and not last else 0))
                    diag = pT[k][:, :, 0:P]
                    g.affine_select(out=diag, in_=diag, compare_op=ALU.is_ge, fill=0.0, base=0,
                                    pattern=[[0, HG], [1, P]], channel_multiplier=-1).then_inc(p_masked, 1)

            mask_group(B_GRP0)
            with pool.Fori(0, B - 1) as b:
                for s in range(NG):
                    mask_group(B_ATT + b * B_PER + s * B_SLOT, split={0: 2 * b + 2, 2: 2 * b + 3}.get(s))
            for s in range(NG - 1):
                mask_group(B_ATT + (B - 1) * B_PER + s * B_SLOT, last=s == NG - 2)

            pool.wait_ge(a_free, A_ALL)
            g.iota(io, [[0, T], [1, E]], base=0, channel_multiplier=0,
                   allow_small_or_imprecise_dtypes=True).then_inc(rconsts, 1)
            g.iota(io8, [[0, T], [1, E]], base=E, channel_multiplier=0,
                   allow_small_or_imprecise_dtypes=True).then_inc(rconsts, 1)
            g.iota(k128, [[0, E], [P, T]], base=0, channel_multiplier=0,
                   allow_small_or_imprecise_dtypes=True).then_inc(rconsts, 1)
            g.iota(tio, [[1, NT], [0, E]], base=0, channel_multiplier=0,
                   allow_small_or_imprecise_dtypes=True).then_inc(rconsts, 1)
            g.memset(upto, 1.0).then_inc(rconsts, 1)
            pool.wait_ge(rconsts, 5)
            g.affine_select(out=upto, in_=upto, compare_op=ALU.is_ge, fill=0.0, base=0,
                            pattern=[[1, E], [-1, E]], channel_multiplier=0).then_inc(rconsts, 1)

            g.iota(xn2[:, :, D:D + 1], [[P, T], [0, 1]], base=0, channel_multiplier=1,
                   allow_small_or_imprecise_dtypes=True).then_inc(rconsts, 1)

            pool.wait_ge(rconsts, 7)
            pool.wait_ge(xg_zeroed, DMA * (NT // Z))
            pool.wait_ge(slots_ready, TOP_K)
            for t in range(T):
                for k in range(TOP_K):
                    g.indirect_dma_start(xg, bass.IndirectOffsetOnAxis(slots[:, k, t:t + 1], 0),
                                         xn2[:, t, :], None).then_inc(scattered, DMA)

            def rows_out(t, a, before):
                if before is not None:
                    pool.wait_ge(*before)
                pool.wait_ge(dst_ready, t + 1)
                pool_turn(e_yr, t + 2)
                g.indirect_dma_start(yc, bass.IndirectOffsetOnAxis(e_dst[:, a:a + 1], 0),
                                     e_y[:, a, :], None).then_inc(e_out[a], DMA)

            rows_out(0, 0, None)
            with pool.Fori(0, (NT - 1) // 2) as i:
                rows_out(2 * i + 1, 1, (e_out[0], DMA * (i + 1)))
                rows_out(2 * i + 2, 0, (e_out[1], DMA * (i + 1)))

        @block.tensor
        def _(pe):
            mm, tr = nc.tensor.matmul, nc.tensor.transpose

            def ln_transposes(b):
                pe.wait_ge(xs_ready, b + 1)
                for c in range(C):
                    for j in range(QT):
                        last = tr(Bk[:, 2 * LN_PAIR[b] + c, j * P:(j + 1) * P],
                                  xs[b % 2][:, j, c * P:(c + 1) * P], ident[:])
                last.then_inc(b_full, 1)

            def rowmax_scores(g, j, n, par):
                pe.wait_ge(a_free, n - 1)
                k, h0, heads = R_JOBS[j]
                w = (k + 1) * P
                in_bank = heads // 2 if k else HG
                for i in range(heads):
                    h = g % 2 * HG + h0 + i
                    dst = pair(A, par)[:, i // in_bank, i % in_bank * w:(i % in_bank + 1) * w]
                    mm(dst, qstack[0:ROWS, g // 2, h, k * P:w], kstack[0:ROWS, g // 2, h, 0:w],
                       start=True, stop=False)
                    last = mm(dst[:, k * P:w], identb[:], maskb[:], start=False, stop=True)
                last.then_inc(a_full, 1)

            def maxima(n, par, g_count, first=False):
                pe.wait_ge(mparts_ready, g_count)
                if not first:
                    pe.wait_ge(b_free, n - 2)
                for k in range(QT):
                    last = mm(bank(par)[0:3 * HG, k * P:(k + 1) * P],
                              mparts[:, k].rearrange("p i h -> p (i h)"), identb[:], start=True, stop=True)
                last.then_inc(b_full, 1)

            def scoresT(g, j, n, par):
                pe.wait_ge(b_free, n - 2)
                k, h0, heads = S_JOBS[j]
                w = S - k * P
                for i in range(heads):
                    h = g % 2 * HG + h0 + i
                    last = mm(bank(par)[:, i * w:(i + 1) * w], kstack[0:ROWS + 3, g // 2, h, k * P:(k + 1) * P],
                              qstack[0:ROWS + 3, g // 2, h, k * P:S], start=True, stop=True)
                last.then_inc(b_full, 1)

            def probs_v(g, count, k):
                if k == 0:
                    pe.wait_ge(pv_free, count)
                pe.wait_ge(p_masked, count * QT + k + 1)
                for h in range(HG):
                    last = mm(pv_bank[32 * h:32 * h + 32, k * P:S], vaug[:, k, HG * g + h, :],
                              pT[k][:, h, :], start=k == 0, stop=k == QT - 1, tile_position=(0, 32 * h))
                if k == QT - 1:
                    last.then_inc(pv_full, 1)

            def project_v(n, par, b, src=cV, tiles=range(QT)):
                if tiles[0] == 0:
                    pe.wait_ge(a_free, n - 1)
                    if src is cV:
                        pe.wait_ge(ld_cv, DMA * b)
                for k in tiles:
                    for c in range(C):
                        last = mm(pair(A, par)[:, k // 2, (k % 2) * D:(k % 2 + 1) * D],
                                  src[:, c, k * P:(k + 1) * P], wv[:, c, :], start=c == 0, stop=c == C - 1)
                if tiles[-1] == QT - 1:
                    last.then_inc(a_full, 1)

            def project(par, a, half, b):
                w, src = ((wq, xnT), (wk, cT))[a]
                for c in range(C):
                    last = mm(pair(A, par)[:, a, :], w[:, c, half * P:(half + 1) * P],
                              src[:, c, bass.ds(b * S, S)], start=c == 0, stop=c == C - 1)
                return last

            pe.wait_ge(ld_k, 2 * DMA)
            for half in range(2):
                project(half, 1, half, 0)
            pe.wait_ge(consts, 1)
            ln_transposes(0)
            pe.wait_ge(b_free, 1)
            pe.wait_ge(ld_q, 3 * DMA)
            for half in range(2):
                project(half, 0, half, 0).then_inc(a_full, 1)
            pe.wait_ge(ld_v, DMA * 2)
            project_v(2, 2, 0, cT)
            pe.wait_ge(consts, 4)
            pe.wait_ge(fills, 3)
            pe.wait_ge(rows_in[0], DMA * 12)
            for j in range(A_GRP):
                rowmax_scores(0, j, 3 + j, 3 + j)
            maxima(MAX_0, B + 2, 1, first=True)
            ln_transposes(1)
            pe.wait_ge(b_free, MAX_0 + 1)
            ln_transposes(2)
            pe.wait_ge(b_free, LN_JOB[1] + 1)
            ln_transposes(3)
            pe.wait_ge(ld_ctx, DMA * (B - 1))
            pe.wait_ge(ld_o, DMA * 2)

            def slot(g, count, n_b, par_b, rows=None, projection=None, wait_rows=None,
                     pv=True):
                at = 0
                if projection:
                    projection(*rows)
                    at = 1
                if wait_rows:
                    pe.wait_ge(*wait_rows)
                for kind, j in SLOT:
                    if kind == "R" and rows:
                        rowmax_scores((g + 1) % NG, j, rows[0] + at + j, rows[1] + at + j)
                    elif kind == "PV" and pv:
                        probs_v((g - 1) % NG, count - 1, j)
                    elif kind == "S":
                        if j == 0:
                            pe.wait_ge(max_in, DMA * (count + 1))
                        skip = 1 if rows and j >= MAX_AT else 0
                        scoresT(g, j, n_b + j + skip, par_b + j + skip)
                    elif kind == "MAX" and rows:
                        maxima(n_b + MAX_AT, par_b + MAX_AT, count + 2)

            pe.wait_ge(b_free, B_GRP0)
            slot(0, 0, B_GRP0, B_GRP0, (3 + A_GRP, 3 + A_GRP), pv=False)
            pe.wait_ge(a_free, A_PRO)

            def ln2_transposes(b):
                pe.wait_ge(xs_ready, B + b + 1)
                for c in range(C):
                    n = B_LN2[b] + c
                    pe.wait_ge(b_free, n - 2)
                    for j in range(QT):
                        last = tr(bank(n)[:, j * P:(j + 1) * P], xn2[:, b * QT + j, c * P:(c + 1) * P], ident[:])
                    last.then_inc(b_full, 1)

            def logits(b):
                if b == 0:
                    pe.wait_ge(ld_moe, DMA * (4 + M))
                if b == B - 1:
                    pe.wait_ge(lt_read, 1)
                pe.wait_ge(b_free, B_LN2[b] + C)
                for c in range(C):
                    last = mm(LOGITS_IN[b][0:E, :], gw[:, c, :], xn2T[:, c, b * S:(b + 1) * S],
                              start=c == 0, stop=c == C - 1)
                last.then_inc(lt_full, 1)

            def logits_t(b):
                pe.wait_ge(lt_read, b + 1)
                for j in range(QT):
                    last = tr(A[:, 2, (b * QT + j) * E:(b * QT + j + 1) * E], lgT[b][:, j * P:(j + 1) * P],
                              ident[0:E, 0:E])
                return last

            def batch(b, final):
                n_a, par_a = A_PRO + b * A_PER, A_PRO
                n_b, par_b = B_ATT + b * B_PER, B_ATT
                count = b * NG

                def next_half(half):
                    def projection(n, par):
                        pe.wait_ge(a_free, n - 1)
                        project(par, 0, half, b + 1)
                        project(par, 1, half, b + 1).then_inc(a_full, 1)
                    return None if final else projection

                for g in range(1, NG):
                    wait_rows = ((rows_in[1], DMA * 12 * (b + 1)) if g == 1 else
                                 (rows_in[0], DMA * 12 * (b + 2)) if g == 3 and not final else None)
                    projection = next_half(g // 2) if g != 2 else None
                    rows = None if final and g == 3 else (n_a, par_a)
                    slot(g, count + g, n_b, par_b, rows, projection, wait_rows)
                    if rows is not None:
                        jobs = A_GRP + (projection is not None)
                        n_a, par_a = n_a + jobs, par_a + jobs
                        n_b, par_b = n_b + 1, par_b + 1
                    n_b, par_b = n_b + S_N, par_b + S_N
                if final:
                    for k in range(QT):
                        probs_v(NG - 1, count + NG - 1, k)
                    ln2_transposes(0)
                    n_b, par_b = n_b + C, par_b + C
                else:
                    slot(0, count + NG, n_b, par_b, (n_a, par_a))
                    n_a, par_a = n_a + A_GRP, par_a + A_GRP
                    n_b, par_b = n_b + B_SLOT, par_b + B_SLOT
                pe.wait_ge(pv_free, count + NG)
                for i in range(2):
                    pe.wait_ge(a_free, n_a - 1)
                    for k in range(2):
                        for g in range(NG):
                            q = 2 * i + k
                            last = tr(pair(A, par_a)[:, k, g * P:(g + 1) * P], oT[:, g, q * P:(q + 1) * P], ident[:])
                    last.then_inc(a_full, 1)
                    n_a, par_a = n_a + 1, par_a + 1
                if not final:
                    project_v(n_a, par_a, b + 1, tiles=range(QT - 1))
                else:
                    ln2_transposes(1)
                    n_b, par_b = n_b + C, par_b + C
                pe.wait_ge(a_free, n_a)
                for tiles in A_TILES:
                    pe.wait_ge(b_free, n_b - 2)
                    for i, ck in enumerate(tiles):
                        c, k = divmod(ck, QT)
                        last = tr(bank(par_b)[:, i * P:(i + 1) * P], attn[:, k, c * P:(c + 1) * P], ident[:])
                    last.then_inc(b_full, 1)
                    n_b, par_b = n_b + 1, par_b + 1
                if final:
                    ln2_transposes(2)
                else:
                    project_v(n_a, par_a, b + 1, tiles=[QT - 1])
                    n_a, par_a = n_a + 1, par_a + 1
                pe.wait_ge(a_free, n_a - 1)
                pe.wait_ge(b_free, n_b)
                for k in range(QT):
                    for c in range(C):
                        last = mm(pair(A, par_a)[:, k // 2, (k % 2) * D:(k % 2 + 1) * D],
                                  attnT[:, c, k * P:(k + 1) * P], wo[:, c, :], start=c == 0, stop=c == C - 1)
                last.then_inc(a_full, 1)
                if not final:
                    pe.wait_ge(a_free, n_a)

            with pe.Fori(0, B - 1) as b:
                batch(b, False)
            batch(B - 1, True)

            gu = [(A[:, 0, :], A[:, 1, :]), (A[:, 2, :], A[:, 3, :]), (Bk[:, 0, :], Bk[:, 1, :])]

            def shared_up(b, lo=0, hi=M):
                for m in range(lo, hi):
                    for w, dst in zip((wsg, wsu), gu[m]):
                        for c in range(C):
                            last = mm(dst, w[:, c, m * P:(m + 1) * P], xn2T[:, c, bass.ds(b * S, S)],
                                      start=c == 0, stop=c == C - 1)
                    last.then_inc(s_up, 1)

            def shared_down(b):
                pe.wait_ge(s_yfree, b + 1)
                for m in range(M):
                    pe.wait_ge(s_h, b * M + m + 1)
                    for j in range(QT):
                        last = mm(Bk[:, 2 + j // 2, (j % 2) * D:(j % 2 + 1) * D], sg[:, m, j * P:(j + 1) * P],
                                  wsd[:, m, :], start=m == 0 and j % 2 == 0, stop=m == M - 1,
                                  skip_group_check=True)
                last.then_inc(s_y, 1)

            for b in range(B - 1):
                logits(b)
            pe.wait_ge(a_free, A_ALL)
            for b in range(B - 2):
                logits_t(b)
            ln2_transposes(B - 1)
            logits_t(B - 2)
            logits(B - 1)
            logits_t(B - 1).then_inc(logits_full, 1)
            shared_up(0, 0, 1)
            pe.wait_ge(sel_ready, 1)
            rank = Bk[:, 2, 0:TE].rearrange("p (t e) -> p t e", e=E)
            mm(rank, beforeb[:], selb, start=True, stop=False, skip_group_check=True)
            for s in range(1, T):
                mm(rank[:, s:T, :], onesb[:], selb[:, 0:T - s, :], start=False, stop=s == T - 1,
                   skip_group_check=True)
            for t in range(T):
                last = mm(Bk[:, 3, 0:E], onesb[:], selb[:, t, :], start=t == 0, stop=t == T - 1)
            last.then_inc(rank_full, 1)
            shared_up(0, 1)
            pe.wait_ge(slots_ready, TOP_K)
            shared_down(0)
            for b in range(1, N_SHARED_1):
                shared_up(b)
                shared_down(b)

            def rows_t(a):
                for c in range(C):
                    last = tr(Bk[:, 0, c * P:(c + 1) * P], e_x[:, a, c * P:(c + 1) * P], ident[:])
                last.then_inc(e_xt, 1)

            def expert(t):
                return pe.value_load(expert_of[0:1, bass.ds(t, 1)], min_val=0, max_val=E - 1)

            def up(t, a, e):
                pe.wait_ge(e_xTr, t + 1)
                for i in range(2):
                    for c in range(C):
                        cols = bass.ds(e * (2 * HALF) + i * HALF, HALF)
                        dst = A[:, 2 * a + i, 0:HALF]
                        mm(dst, e_xT_hi[:, a, c, :], wup_hi[:, c, cols], start=c == 0, stop=False)
                        mm(dst, e_xT_hi[:, a, c, :], wup_lo[:, c, cols], start=False, stop=False)
                        last = mm(dst, e_xT_lo[:, a, c, :], wup_hi[:, c, cols], start=False, stop=c == C - 1)
                last.then_inc(e_up, 1)

            def hidden_t(t, a):
                pe.wait_ge(e_hr, t + 1)
                for m in range(M):
                    last = tr(Bk[:, 1, m * P:(m + 1) * P], e_h[:, a, m * P:(m + 1) * P], ident[:])
                last.then_inc(e_ht, 1)

            def down(t, a, e, load=None):
                pe.wait_ge(e_hTr, t + 1)
                pe.wait_ge(e_yr, t + 1)
                for m in range(M):
                    last = mm(Bk[:, 2, 0:D], e_hT[:, a, m, :], wdn[:, m, bass.ds(e * D, D)],
                              start=m == 0, stop=m == M - 1)
                    if m == 1 and load is not None:
                        e_next = expert(load)
                last.then_inc(e_yf, 1)
                return e_next if load is not None else None

            pe.wait_ge(up_lo, SPLITS)
            pe.wait_ge(experts_known, 1)
            pe.wait_ge(e_in[0], DMA)
            rows_t(0)
            pe.wait_ge(e_in[1], DMA)
            pe.wait_ge(e_xTr, 1)
            rows_t(1)
            up(0, 0, expert(0))
            up(1, 1, expert(1))
            hidden_t(0, 0)
            pe.wait_ge(s_yfree, N_SHARED_1 + 1)
            pe.wait_ge(e_in[0], 2 * DMA)
            rows_t(0)
            up(2, 0, expert(2))
            with pe.Fori(0, (NT - 3) // 2) as i:
                t = 2 * i + 1
                for a in (1, 0):
                    pe.wait_ge(e_hTr, t)
                    hidden_t(t, a)
                    e_down = expert(t - 1)
                    pe.wait_ge(e_in[a], DMA * (i + (2 if a else 3)))
                    rows_t(a)
                    e_next = down(t - 1, 1 - a, e_down, t + 2)
                    up(t + 2, a, e_next)
                    t = t + 1
            e_last = [expert(t) for t in range(NT - 3, NT)]
            pe.wait_ge(e_hTr, NT - 2)
            hidden_t(NT - 2, 1)
            down(NT - 3, 0, e_last[0])
            pe.wait_ge(e_hTr, NT - 1)
            hidden_t(NT - 1, 0)
            down(NT - 2, 1, e_last[1])
            down(NT - 1, 0, e_last[2])
            pe.wait_ge(e_hTr, NT)
            pe.wait_ge(e_yr, NT + 1)
            for b in range(N_SHARED_1, B):
                shared_up(b)
                shared_down(b)

        @block.scalar
        def _(act):
            copy = lambda o, i: nc.scalar.activation(o, i, ACT.Copy)

            def deviations(i, lo, hi):
                act.wait_ge(ln_step, 5 * (i + 1))
                nc.scalar.activation(std[:, lo:hi], st_a[:, lo:hi], ACT.Sqrt).then_inc(std_ready, 1)

            deviations(0, 0, QT)

            def part1(u, n, w):
                if w is not None:
                    act.wait_ge(*w)
                for a in range(2):
                    act.wait_ge(*((val_ready, u + 1), (a_free, n + 1))[a])
                    copy(parts[:, a, 0, :], val[:, a, :]).then_inc(part1_ready, 1)

            def part2(u):
                for a in range(2):
                    act.wait_ge(rem_ready, 2 * u + a + 1)
                    copy(parts[:, a, 1, :], rem[:, a, :]).then_inc(part2_ready, 1)

            def ln_copy(b):
                act.wait_ge(b_full, LN_JOB[b] + 1)
                copy(xnT[:, :, b * S:(b + 1) * S], pair(Bk, LN_PAIR[b])).then_inc(b_free, 1)

            ln_copy(0)
            part1(0, 0, None)
            part2(0)
            deviations(1, QT, T)
            part1(1, 1, (rows_in[0], DMA * 12))
            part2(1)

            def max_rows(n, par):
                act.wait_ge(b_full, n + 1)
                copy(mrows[0:3 * HG, :], bank(par)[0:3 * HG, :]).then_inc(b_free, 1)

            def exps(n, par, pv=None, rows=True, split=None):
                for j, (k, h, heads) in enumerate(S_JOBS):
                    if pv and j == MAX_AT:
                        p_v(*pv)
                    if rows and j == MAX_AT:
                        max_rows(n, par)
                        n, par = n + 1, par + 1
                    act.wait_ge(b_full, n + 1)
                    nc.scalar.activation(pT[k][:, h:h + heads, :], bank(par)[:, 0:heads * (S - k * P)],
                                         ACT.Exp).then_inc(b_free, 1)
                    n, par = n + 1, par + 1
                    if split is not None and (k, h + heads) == (1, HG):
                        part2(split)
                return n, par

            def ln2_copies(b):
                for c in range(C):
                    n = B_LN2[b] + c
                    act.wait_ge(b_full, n + 1)
                    copy(xn2T[:, c, b * S:(b + 1) * S], bank(n)).then_inc(b_free, 1)

            def p_v(g, count):
                act.wait_ge(pv_full, count + 1)
                copy(oT[:, g, :], pv_bank).then_inc(pv_free, 1)

            def batch(b, final):
                n, par = B_ATT + b * B_PER, B_ATT
                n_a = A_PRO + b * A_PER
                count = b * NG
                for g in range(1, NG):
                    u = None
                    if g != 2 and not final:
                        u, job = (2 * b + 2, n_a) if g == 1 else (2 * b + 3, n_a + 2 * A_GRP + 1)
                        part1(u, job, (rows_in[1], DMA * 12 * (b + 1)) if g == 1 else
                              (rows_in[0], DMA * 12 * (b + 2)))
                    n, par = exps(n, par, (g - 1, count + g - 1), not (final and g == NG - 1), u)
                if final:
                    deviations(2, 0, T - QT)
                    p_v(NG - 1, count + NG - 1)
                    ln2_copies(0)
                    ln2_copies(1)
                    n, par = n + 2 * C, par + 2 * C
                else:
                    n, par = exps(n, par, (NG - 1, count + NG - 1))
                for tiles in A_TILES:
                    act.wait_ge(b_full, n + 1)
                    w = len(tiles) * P
                    copy(attnT.rearrange("p c n -> p (c n)")[:, tiles[0] * P:tiles[0] * P + w],
                         bank(par)[:, 0:w]).then_inc(b_free, 1)
                    n, par = n + 1, par + 1

            max_rows(MAX_0, B + 2)
            for b in range(1, B):
                ln_copy(b)
            exps(B_GRP0, B_GRP0)
            with act.Fori(0, B - 1) as b:
                batch(b, False)
            batch(B - 1, True)

            def logits_copy(b):
                act.wait_ge(lt_full, b + 1)
                copy(lgT[b], LOGITS_IN[b][0:E, :]).then_inc(lt_read, 1)

            ln2_copies(2)
            logits_copy(0)
            logits_copy(1)
            deviations(3, T - QT, T)
            logits_copy(2)
            ln2_copies(3)
            logits_copy(3)

            act.wait_ge(d_ready, 1)
            nc.scalar.activation(ex, dl, ACT.Exp).then_inc(ex_ready, 1)
            gate = [A[:, 0, :], A[:, 2, :], Bk[:, 0, :]]

            def shared_silu(b):
                for m in range(M):
                    act.wait_ge(s_up, b * M + m + 1)
                    nc.scalar.activation(sg[:, m, :], gate[m], ACT.Silu).then_inc(s_sg, 1)

            for b in range(N_SHARED_1):
                shared_silu(b)
                if b == 0:
                    act.wait_ge(ld_up, DMA * C)
                    act.wait_ge(wts_ready, 1)
                for i in SPLIT_AT[b]:
                    copy(piece(wup_hi, i), piece(wup, i)).then_inc(up_hi, 1)

            def rows_t(t, a):
                act.wait_ge(e_xt, t + 1)
                copy(e_xT_hi[:, a], Bk[:, 0, 0:C * P].rearrange("p (c n) -> p c n", c=C)).then_inc(e_xhi, 1)

            def silu(t, a):
                act.wait_ge(e_up, t + 1)
                nc.scalar.activation(e_sg[:, a, :], A[:, 2 * a, 0:HALF], ACT.Silu).then_inc(e_sgr, 1)

            def hidden_t(t, a):
                act.wait_ge(e_ht, t + 1)
                copy(e_hT[:, a], Bk[:, 1, 0:M * P].rearrange("p (c n) -> p c n", c=M)).then_inc(e_hTr, 1)

            rows_t(0, 0)
            rows_t(1, 1)
            silu(0, 0)
            silu(1, 1)
            hidden_t(0, 0)
            rows_t(2, 0)
            silu(2, 0)
            with act.Fori(0, (NT - 3) // 2) as i:
                t = 2 * i + 1
                hidden_t(t, 1)
                rows_t(t + 2, 1)
                silu(t + 2, 1)
                hidden_t(t + 1, 0)
                rows_t(t + 3, 0)
                silu(t + 3, 0)
            hidden_t(NT - 2, 1)
            hidden_t(NT - 1, 0)
            for b in range(N_SHARED_1, B):
                shared_silu(b)

        @block.vector
        def _(dve):
            v = nc.vector

            def moments(i, lo, hi, seen):
                me, mo, qe, qo = (stats[:, lo:hi, k] for k in (1, 4, 2, 5))
                mean_, a, c = mean[:, lo:hi], st_a[:, lo:hi], st_c[:, lo:hi]
                dve.wait_ge(st_done, seen)
                v.tensor_tensor(mean_, me, mo, ALU.add).then_inc(ln_step, 1)
                v.tensor_tensor(c, qe, qo, ALU.add).then_inc(ln_step, 1)
                v.tensor_tensor(a, me, mo, ALU.subtract).then_inc(ln_step, 1)
                dve.wait_ge(ln_step, 5 * i + 3)
                v.scalar_tensor_tensor(out=a, in0=a, scalar=0.25, in1=a, op0=ALU.mult,
                                       op1=ALU.mult).then_inc(ln_step, 1)
                v.tensor_scalar(mean_, mean_, 0.5, None, ALU.mult).then_inc(mean_done, 1)
                v.tensor_scalar(c, c, 1.0 / D, EPS, ALU.mult, ALU.add).then_inc(mean_done, 1)
                dve.wait_ge(ln_step, 5 * i + 4)
                dve.wait_ge(mean_done, 3 * i + 2)
                v.tensor_tensor(a, a, c, ALU.add).then_inc(ln_step, 1)
                dve.wait_ge(std_ready, i + 1)
                v.reciprocal(rstd[:, lo:hi], std[:, lo:hi]).then_inc(mean_done, 1)
                dve.wait_ge(mean_done, 3 * i + 3)

            def normalised(b, dst):
                for j in range(QT):
                    t = b * QT + j
                    last = v.tensor_scalar(dst(j), xs_all[:, bass.ds(t, 1), :], mean[:, bass.ds(t, 1)],
                                           rstd[:, bass.ds(t, 1)], ALU.subtract, ALU.mult)
                return last

            def statistics(b):
                dve.wait_ge(ld_x[b], DMA)
                for j in range(QT):
                    v.bn_stats(stats[:, b * QT + j, :], xs_all[:, b * QT + j, :]).then_inc(st_done, 1)

            def values(n, half, par):
                dve.wait_ge(a_full, n + 1)
                for a, (bias, scale) in enumerate(((bqc, SCALE), (bkc, 1.0))):
                    last = v.tensor_scalar(val[:, a, :], pair(A, par)[:, a, :], bias[:, half:half + 1], scale,
                                           ALU.add, ALU.mult)
                    last.then_inc(a_free if a else val_ready, 1)

            def remainders(u):
                for a in range(2):
                    dve.wait_ge(part1_ready, 2 * u + a + 1)
                    v.tensor_tensor(rem[:, a, :], val[:, a, :], parts[:, a, 0, :], ALU.subtract).then_inc(rem_ready, 1)

            def part3(u):
                for a in range(2):
                    dve.wait_ge(part2_ready, 2 * u + a + 1)
                    last = v.tensor_tensor(parts[:, a, 2, :], rem[:, a, :], parts[:, a, 1, :], ALU.subtract)
                    last.then_inc(parts_ready, 1)

            statistics(0)
            moments(0, 0, QT, QT)
            normalised(0, lambda j: xs[0][:, j:j + 1, :]).then_inc(xs_ready, 1)
            statistics(1)
            values(0, 0, 0)
            remainders(0)
            part3(0)
            values(1, 1, 1)

            def add_v(n, par):
                dve.wait_ge(a_full, n + 1)
                vv = pair(A, par).rearrange("p a (k h i) -> p (a k) h i", k=2, h=H)
                bb = bv_bc.rearrange("p (o h i) -> p o h i", o=1, h=H).to_broadcast([P, QT, H, DK])
                v.tensor_tensor(vaug[:, :, :, 0:DK], vv, bb, ALU.add).then_inc(a_free, 1)

            dve.wait_ge(fills, 3)
            dve.wait_ge(ld_v, DMA * 2)
            add_v(2, 2)
            for b in range(2, B):
                statistics(b)
            moments(1, QT, T, T)
            normalised(1, lambda j: xs[1][:, j:j + 1, :]).then_inc(xs_ready, 1)

            def rowmax(j, n, par):
                k, h, heads = R_JOBS[j]
                dve.wait_ge(a_full, n + 1)
                if k:
                    src = pair(A, par)[:, :, 0:heads // 2 * (k + 1) * P].rearrange("p a (h n) -> p a h n",
                                                                                 h=heads // 2)
                    dst = mneg[:, k, h:h + heads].rearrange("p (a h) -> p a h", a=2)
                else:
                    src = pair(A, par)[:, 0, :].rearrange("p (h n) -> p h n", h=HG)
                    dst = mneg[:, k, :]
                v.tensor_reduce(dst, src, AX.X, ALU.max, negate=True).then_inc(a_free, 1)

            def max_parts(n, g_count):
                dve.wait_ge(a_free, n)
                s0 = (g_count - 1) * 3
                v.tensor_copy(mparts[:, :, 0, :], mneg).then_inc(mpart_step, 1)
                dve.wait_ge(mpart_step, s0 + 1)
                v.tensor_tensor(mrem, mneg, mparts[:, :, 0, :], ALU.subtract).then_inc(mpart_step, 1)
                dve.wait_ge(mpart_step, s0 + 2)
                v.tensor_copy(mparts[:, :, 1, :], mrem).then_inc(mpart_step, 1)
                dve.wait_ge(mpart_step, s0 + 3)
                v.tensor_tensor(mparts[:, :, 2, :], mrem, mparts[:, :, 1, :], ALU.subtract).then_inc(mparts_ready, 1)

            for g in range(2):
                for j in range(A_GRP):
                    n = 3 + g * A_GRP + j
                    rowmax(j, n, n)
                    if g == 0 and j == 1:
                        remainders(1)
                    if g == 0 and j == 3:
                        part3(1)
                max_parts(3 + (g + 1) * A_GRP, g + 1)
                if g == 0:
                    for b in range(2, B):
                        dve.wait_ge(b_full, LN_JOB[b - 2] + 1)
                        normalised(b, lambda j: xs[b % 2][:, j:j + 1, :]).then_inc(xs_ready, 1)

            def batch(b, final):
                n, par = A_PRO + b * A_PER, A_PRO
                for g in range(1, NG + 1):
                    splits = g in (1, 3) and not final
                    if final and g >= NG - 1:
                        break
                    for j in range(A_GRP):
                        if splits and j == 0:
                            values(n, g // 2, par)
                            n, par = n + 1, par + 1
                        rowmax(j, n, par)
                        n, par = n + 1, par + 1
                    max_parts(n, b * NG + g + 2)
                if final:
                    moments(2, 0, T - QT, 2 * T - QT)
                    normalised(0, ln2_row(0)).then_inc(xs_ready, 1)
                    normalised(1, ln2_row(1)).then_inc(xs_ready, 1)
                for i in range(2):
                    dve.wait_ge(a_full, n + 1)
                    o = pair(A, par).rearrange("p k (h w) -> p k h w", w=32)
                    rci = rc[:, 2 * i:2 * i + 2, :]
                    v.reciprocal(rci, o[:, :, :, DK]).then_inc(rc_ready, 1)
                    dve.wait_ge(rc_ready, 2 * b + i + 1)
                    v.tensor_tensor(attn[:, 2 * i:2 * i + 2, :].rearrange("p k (h i) -> p k h i", h=H),
                                    o[:, :, :, 0:DK],
                                    rci.rearrange("p k (h o) -> p k h o", o=1).to_broadcast([P, 2, H, DK]),
                                    ALU.mult).then_inc(a_free, 1)
                    n, par = n + 1, par + 1
                if not final:
                    add_v(n, par)
                    n, par = n + 1, par + 1
                if final:
                    normalised(2, ln2_row(2)).then_inc(xs_ready, 1)
                dve.wait_ge(a_full, n + 1)
                rows = xs_all[:, bass.ds(b * QT, QT), :]
                v.tensor_tensor(rows, pair(A, par).rearrange("p a (k d) -> p (a k) d", k=2), rows,
                                ALU.add).then_inc(a_free, 1)
                dve.wait_ge(a_free, n + 1)
                for j in range(QT):
                    v.bn_stats(stats[:, bass.ds(b * QT + j, 1), :],
                               xs_all[:, bass.ds(b * QT + j, 1), :]).then_inc(st_done, 1)

            def ln2_row(b):
                return lambda j: xn2[:, b * QT + j:b * QT + j + 1, 0:D]

            dve.wait_ge(bo_added, 1)
            with dve.Fori(0, B - 1) as b:
                batch(b, False)
            batch(B - 1, True)

            moments(3, T - QT, T, 2 * T)
            normalised(3, ln2_row(3)).then_inc(xs_ready, 1)

            steps = [0]

            def link(ins):
                steps[0] += 1
                ins.then_inc(route, 1)
                dve.wait_ge(route, steps[0])

            def over_e(col):
                return col.rearrange("p (t o) -> p t o", o=1).to_broadcast([P, T, E])

            dve.wait_ge(logits_full, 1)
            dve.wait_ge(rconsts, 6)
            v.tensor_copy(lg, A[:, 2, 0:TE].rearrange("p (t e) -> p t e", e=E)).then_inc(lg_read, 1)
            dve.wait_ge(lg_read, 1)

            def shared_h(b, m):
                dve.wait_ge(s_sg, b * M + m + 1)
                up_ = (A[:, 1, :], A[:, 3, :], Bk[:, 1, :])[m]
                v.tensor_tensor(sg[:, m, :], up_, sg[:, m, :], ALU.mult).then_inc(s_h, 1)

            def shared_y(b):
                dve.wait_ge(s_y, b + 1)
                rows = xs_all[:, bass.ds(b * QT, QT), :]
                v.tensor_tensor(rows, Bk[:, 2:4, :].rearrange("p a (k d) -> p (a k) d", k=2), rows,
                                ALU.add).then_inc(s_yfree, 1)

            link(v.tensor_reduce(m1, lg, AX.X, ALU.max))
            link(v.tensor_tensor(ra, lg, over_e(m1), ALU.is_equal))
            link(v.scalar_tensor_tensor(out=ra, in0=ra, scalar=-float(E), in1=io8, op0=ALU.mult, op1=ALU.add))
            link(v.tensor_reduce(i1, ra, AX.X, ALU.min))
            link(v.tensor_tensor(oh1, io, over_e(i1), ALU.is_equal))
            link(v.scalar_tensor_tensor(out=rb, in0=oh1, scalar=LOWEST, in1=lg, op0=ALU.mult, op1=ALU.add))
            link(v.tensor_reduce(m2, rb, AX.X, ALU.max))
            link(v.tensor_tensor(ra, rb, over_e(m2), ALU.is_equal))
            link(v.scalar_tensor_tensor(out=ra, in0=ra, scalar=-float(E), in1=io8, op0=ALU.mult, op1=ALU.add))
            link(v.tensor_reduce(i2, ra, AX.X, ALU.min))
            link(v.tensor_tensor(oh2, io, over_e(i2), ALU.is_equal))
            v.tensor_tensor(dl, m2, m1, ALU.subtract).then_inc(d_ready, 1)
            link(v.tensor_copy(xn2[:, :, D + 1:D + 2], i1.rearrange("p (t o) -> p t o", o=1)))
            v.tensor_tensor(selb, oh1, oh2, ALU.add).then_inc(sel_ready, 1)
            dve.wait_ge(rank_full, 1)
            link(v.tensor_copy(tot, Bk[:, 3, 0:E]))
            link(v.tensor_tensor(k128, tot.rearrange("p (e o) -> p e o", o=1).to_broadcast([P, E, T]), k128,
                                 ALU.is_gt))
            link(v.tensor_reduce(tiles_of, k128, AX.X, ALU.add))
            link(v.tensor_tensor(ee, tiles_of.rearrange("p (o e) -> p o e", o=1).to_broadcast([P, E, E]), upto,
                                 ALU.mult))
            link(v.tensor_reduce(ends, ee, AX.X, ALU.add))
            link(v.tensor_tensor(base, ends, tiles_of, ALU.subtract))
            link(v.scalar_tensor_tensor(
                out=rslot, in0=base.rearrange("p (o e) -> p o e", o=1).to_broadcast([P, T, E]), scalar=float(P),
                in1=Bk[:, 2, 0:TE].rearrange("p (t e) -> p t e", e=E), op0=ALU.mult, op1=ALU.add))
            link(v.tensor_tensor(tcmp, ends.rearrange("p (o e) -> p o e", o=1).to_broadcast([P, NT, E]), tio,
                                 ALU.is_le))
            link(v.tensor_reduce(tnum, tcmp, AX.X, ALU.add))
            link(v.tensor_scalar(expert_f[:], tnum, float(E - 1), None, ALU.min))
            v.tensor_copy(expert_of[:], expert_f[:]).then_inc(experts_known, 1)
            for k, oh in enumerate((oh1, oh2)):
                link(v.tensor_tensor(oh, oh, rslot, ALU.mult))
                link(v.tensor_reduce(slotf[:, k, :], oh, AX.X, ALU.add))
                v.tensor_copy(slots[:, k, :], slotf[:, k, :]).then_inc(slots_ready, 1)

            dve.wait_ge(ex_ready, 1)
            link(v.tensor_scalar(sm, ex, 1.0, None, ALU.add))
            link(v.reciprocal(wts[:, 0, :], sm))
            v.tensor_tensor(wts[:, 1, :], ex, wts[:, 0, :], ALU.mult).then_inc(wts_ready, 1)
            for b in range(N_SHARED_1):
                for m in range(M):
                    shared_h(b, m)
                shared_y(b)
                for i in SPLIT_AT[b]:
                    dve.wait_ge(up_hi, i + 1)
                    v.tensor_tensor(piece(wup_lo, i), piece(wup, i), piece(wup_hi, i),
                                    ALU.subtract).then_inc(up_lo, 1)

            def rows_lo(t, a):
                dve.wait_ge(e_xhi, t + 1)
                v.tensor_tensor(e_xT_lo[:, a], Bk[:, 0, 0:C * P].rearrange("p (c n) -> p c n", c=C),
                                e_xT_hi[:, a], ALU.subtract).then_inc(e_xTr, 1)

            def hidden(t, a):
                dve.wait_ge(e_sgr, t + 1)
                v.tensor_tensor(e_h[:, a, :], A[:, 2 * a + 1, 0:HALF], e_sg[:, a, :], ALU.mult).then_inc(e_hr, 1)

            def result(t, a, i, wait=True):
                if wait:
                    dve.wait_ge(e_out[a], DMA * i)
                dve.wait_ge(who_in[a], DMA * (i + 1))
                v.tensor_scalar(e_second[:, a:a + 1], e_who[:, a, 1:2], expert_f[:, bass.ds(t, 1)], float(N),
                                ALU.not_equal, ALU.mult).then_inc(second, 1)
                dve.wait_ge(second, t + 1)
                v.tensor_tensor(e_dst[:, a:a + 1], e_second[:, a:a + 1], e_who[:, a, 0:1],
                                ALU.add).then_inc(dst_ready, 1)
                dve.wait_ge(e_yf, t + 1)
                v.tensor_copy(e_y[:, a, :], Bk[:, 2, 0:D]).then_inc(e_yr, 1)

            rows_lo(0, 0)
            rows_lo(1, 1)
            hidden(0, 0)
            hidden(1, 1)
            rows_lo(2, 0)
            hidden(2, 0)

            def pair_of_tiles(i, wait):
                t = 2 * i + 1
                rows_lo(t + 2, 1)
                result(t - 1, 0, i, wait)
                hidden(t + 2, 1)
                rows_lo(t + 3, 0)
                result(t, 1, i, wait)
                hidden(t + 3, 0)

            pair_of_tiles(0, False)
            with dve.Fori(1, (NT - 3) // 2) as i:
                pair_of_tiles(i, True)
            result(NT - 3, 0, (NT - 3) // 2)
            result(NT - 2, 1, (NT - 3) // 2)
            result(NT - 1, 0, (NT - 1) // 2)

            def combine(t):
                dve.wait_ge(y_in[t % NYB], DMA * (t // NYB + 1))
                row = xs_all[:, t, :]
                v.scalar_tensor_tensor(out=row, in0=yb[t % NYB][:, 0, :], scalar=wts[:, 0, t:t + 1], in1=row,
                                       op0=ALU.mult, op1=ALU.add).then_inc(comb1, 1)
                dve.wait_ge(comb1, t + 1)
                v.scalar_tensor_tensor(out=row, in0=yb[t % NYB][:, 1, :], scalar=wts[:, 1, t:t + 1], in1=row,
                                       op0=ALU.mult, op1=ALU.add).then_inc(comb2, 1)

            t = 0
            for b in range(N_SHARED_1, B):
                for m in range(M):
                    shared_h(b, m)
                    combine(t)
                    combine(t + 1)
                    t += 2
            for t in range(t, N_SHARED_1 * QT):
                combine(t)
            for b in range(N_SHARED_1, B):
                shared_y(b)
            dve.wait_ge(s_yfree, B + 1)
            for t in range(N_SHARED_1 * QT, T):
                combine(t)


def kernel(x, ctx_1024, L0_xattn_Wq, L0_xattn_bq, L0_xattn_Wk, L0_xattn_bk, L0_xattn_Wv, L0_xattn_bv,
           L0_xattn_Wo, L0_xattn_bo, L0_ffn_gate_w, L0_ffn_w_up, L0_ffn_w_down, L0_ffn_sg_gate,
           L0_ffn_sg_up, L0_ffn_sg_down):
    import numpy as np
    import concourse.bacc as bacc
    from concourse.bass_utils import run_bass_kernel_spmd

    def by_half(a):
        return np.transpose(np.reshape(a, (-1, 2, NUM_HEADS // 2, a.shape[-1] // NUM_HEADS)),
                            (0, 1, 3, 2)).reshape(-1, a.shape[-1])

    arrays = {
        "x": x,
        "ctxT": np.transpose(ctx_1024, (0, 2, 1)),
        "wqT": by_half(np.transpose(L0_xattn_Wq)), "bq": np.transpose(by_half(L0_xattn_bq).reshape(2, -1)),
        "wkT": by_half(np.transpose(L0_xattn_Wk)), "bk": np.transpose(by_half(L0_xattn_bk).reshape(2, -1)),
        "wvT": np.transpose(L0_xattn_Wv), "bv": L0_xattn_bv,
        "woT": np.transpose(L0_xattn_Wo), "bo": L0_xattn_bo,
        "gwT": np.transpose(L0_ffn_gate_w),
        "wupT": np.transpose(L0_ffn_w_up, (2, 0, 1)).reshape(L0_ffn_w_up.shape[2], -1),
        "wdnT": np.transpose(L0_ffn_w_down, (2, 0, 1)).reshape(L0_ffn_w_down.shape[2], -1),
        "sgT": np.transpose(L0_ffn_sg_gate),
        "suT": np.transpose(L0_ffn_sg_up),
        "sdT": np.transpose(L0_ffn_sg_down),
    }
    arrays = {k: np.ascontiguousarray(v) for k, v in arrays.items()}
    nc = bacc.Bacc("TRN2", target_bir_lowering=False, num_devices=1)
    aps = {k: nc.dram_tensor(f"in_{k}", a.shape, mybir.dt.from_np(a.dtype), kind="ExternalInput").ap()
           for k, a in arrays.items()}
    out = nc.dram_tensor("out", x.shape, mybir.dt.from_np(np.dtype(x.dtype)), kind="ExternalOutput").ap()
    build(nc, *aps.values(), out)
    r = run_bass_kernel_spmd(nc, [{f"in_{k}": a for k, a in arrays.items()}], core_ids=[0])
    return r.results[0]["out"]
```
